# Optimizing a Trainium2 kernel written in Bass

```python
import numpy as np
import jax
import jax.numpy as jnp

def _softmax(x, axis=-1):
    return jax.nn.softmax(x, axis=axis)

def _gelu(x):
    return jax.nn.gelu(x, approximate=True)

def _silu(x):
    return jax.nn.silu(x)

def _sigmoid(x):
    return jax.nn.sigmoid(x)

def _layernorm(x, axis=-1, eps=1e-05):
    m = jnp.mean(x, axis=axis, keepdims=True)
    v = jnp.var(x, axis=axis, keepdims=True)
    return (x - m) / jnp.sqrt(v + eps)

def _scatter_add(tgt, idx, src, axis=0):
    return tgt.at[idx].add(src)

def _segment_sum(src, seg, n):
    return jax.ops.segment_sum(src, seg, n)
kernel_name = 'mk_dlrm_tower_d1_rec_r8_d5c9ba'

def setup_inputs(seed: int=0):
    np.random.seed(seed)
    _w = jnp.asarray

    def _rec_inputs():
        import jax
        import jax.numpy as jnp
        _tk = jax.random.key(seed)
        dense_ctx = jax.random.normal(jax.random.fold_in(_tk, 190), (512, 16), jnp.float32)
        ids = jnp.stack([jax.random.randint(jax.random.fold_in(_tk, 200 + f), (512,), 0, v, jnp.int32) for f, v in enumerate([1250, 1250, 12500, 12500, 1250, 1000, 12500, 125000, 1250, 125000, 1000, 1000, 1000, 1000, 12500, 1000, 125000, 12500, 12500, 1000, 125000, 1250, 125000, 1000, 1250, 12500, 1000, 1250, 125000, 12500, 12500, 1250, 1000, 1250, 1250, 12500, 1000, 1250, 12500, 1000])], axis=1)
        tbl_0 = 0.05 * jax.random.normal(jax.random.fold_in(_tk, 500 + 0), (1250, 32), jnp.float32)
        tbl_1 = 0.05 * jax.random.normal(jax.random.fold_in(_tk, 500 + 1), (1250, 32), jnp.float32)
        tbl_2 = 0.05 * jax.random.normal(jax.random.fold_in(_tk, 500 + 2), (12500, 32), jnp.float32)
        tbl_3 = 0.05 * jax.random.normal(jax.random.fold_in(_tk, 500 + 3), (12500, 32), jnp.float32)
        tbl_4 = 0.05 * jax.random.normal(jax.random.fold_in(_tk, 500 + 4), (1250, 32), jnp.float32)
        tbl_5 = 0.05 * jax.random.normal(jax.random.fold_in(_tk, 500 + 5), (1000, 32), jnp.float32)
        tbl_6 = 0.05 * jax.random.normal(jax.random.fold_in(_tk, 500 + 6), (12500, 32), jnp.float32)
        tbl_7 = 0.05 * jax.random.normal(jax.random.fold_in(_tk, 500 + 7), (125000, 32), jnp.float32)
        tbl_8 = 0.05 * jax.random.normal(jax.random.fold_in(_tk, 500 + 8), (1250, 32), jnp.float32)
        tbl_9 = 0.05 * jax.random.normal(jax.random.fold_in(_tk, 500 + 9), (125000, 32), jnp.float32)
        tbl_10 = 0.05 * jax.random.normal(jax.random.fold_in(_tk, 500 + 10), (1000, 32), jnp.float32)
        tbl_11 = 0.05 * jax.random.normal(jax.random.fold_in(_tk, 500 + 11), (1000, 32), jnp.float32)
        tbl_12 = 0.05 * jax.random.normal(jax.random.fold_in(_tk, 500 + 12), (1000, 32), jnp.float32)
        tbl_13 = 0.05 * jax.random.normal(jax.random.fold_in(_tk, 500 + 13), (1000, 32), jnp.float32)
        tbl_14 = 0.05 * jax.random.normal(jax.random.fold_in(_tk, 500 + 14), (12500, 32), jnp.float32)
        tbl_15 = 0.05 * jax.random.normal(jax.random.fold_in(_tk, 500 + 15), (1000, 32), jnp.float32)
        tbl_16 = 0.05 * jax.random.normal(jax.random.fold_in(_tk, 500 + 16), (125000, 32), jnp.float32)
        tbl_17 = 0.05 * jax.random.normal(jax.random.fold_in(_tk, 500 + 17), (12500, 32), jnp.float32)
        tbl_18 = 0.05 * jax.random.normal(jax.random.fold_in(_tk, 500 + 18), (12500, 32), jnp.float32)
        tbl_19 = 0.05 * jax.random.normal(jax.random.fold_in(_tk, 500 + 19), (1000, 32), jnp.float32)
        tbl_20 = 0.05 * jax.random.normal(jax.random.fold_in(_tk, 500 + 20), (125000, 32), jnp.float32)
        tbl_21 = 0.05 * jax.random.normal(jax.random.fold_in(_tk, 500 + 21), (1250, 32), jnp.float32)
        tbl_22 = 0.05 * jax.random.normal(jax.random.fold_in(_tk, 500 + 22), (125000, 32), jnp.float32)
        tbl_23 = 0.05 * jax.random.normal(jax.random.fold_in(_tk, 500 + 23), (1000, 32), jnp.float32)
        tbl_24 = 0.05 * jax.random.normal(jax.random.fold_in(_tk, 500 + 24), (1250, 32), jnp.float32)
        tbl_25 = 0.05 * jax.random.normal(jax.random.fold_in(_tk, 500 + 25), (12500, 32), jnp.float32)
        tbl_26 = 0.05 * jax.random.normal(jax.random.fold_in(_tk, 500 + 26), (1000, 32), jnp.float32)
        tbl_27 = 0.05 * jax.random.normal(jax.random.fold_in(_tk, 500 + 27), (1250, 32), jnp.float32)
        tbl_28 = 0.05 * jax.random.normal(jax.random.fold_in(_tk, 500 + 28), (125000, 32), jnp.float32)
        tbl_29 = 0.05 * jax.random.normal(jax.random.fold_in(_tk, 500 + 29), (12500, 32), jnp.float32)
        tbl_30 = 0.05 * jax.random.normal(jax.random.fold_in(_tk, 500 + 30), (12500, 32), jnp.float32)
        tbl_31 = 0.05 * jax.random.normal(jax.random.fold_in(_tk, 500 + 31), (1250, 32), jnp.float32)
        tbl_32 = 0.05 * jax.random.normal(jax.random.fold_in(_tk, 500 + 32), (1000, 32), jnp.float32)
        tbl_33 = 0.05 * jax.random.normal(jax.random.fold_in(_tk, 500 + 33), (1250, 32), jnp.float32)
        tbl_34 = 0.05 * jax.random.normal(jax.random.fold_in(_tk, 500 + 34), (1250, 32), jnp.float32)
        tbl_35 = 0.05 * jax.random.normal(jax.random.fold_in(_tk, 500 + 35), (12500, 32), jnp.float32)
        tbl_36 = 0.05 * jax.random.normal(jax.random.fold_in(_tk, 500 + 36), (1000, 32), jnp.float32)
        tbl_37 = 0.05 * jax.random.normal(jax.random.fold_in(_tk, 500 + 37), (1250, 32), jnp.float32)
        tbl_38 = 0.05 * jax.random.normal(jax.random.fold_in(_tk, 500 + 38), (12500, 32), jnp.float32)
        tbl_39 = 0.05 * jax.random.normal(jax.random.fold_in(_tk, 500 + 39), (1000, 32), jnp.float32)
        _rk = jax.random.fold_in(_tk, 7)
        W_top1 = 0.0354441 * jax.random.normal(jax.random.fold_in(_tk, 801), (796, 512), jnp.float32)
        W_top2 = 0.0441942 * jax.random.normal(jax.random.fold_in(_tk, 802), (512, 256), jnp.float32)
        W_top3 = 0.0625 * jax.random.normal(jax.random.fold_in(_tk, 803), (256, 1), jnp.float32)
        b_top1 = jnp.zeros((512,), jnp.float32)
        b_top2 = jnp.zeros((256,), jnp.float32)
        return (dense_ctx, ids, tbl_0, tbl_1, tbl_2, tbl_3, tbl_4, tbl_5, tbl_6, tbl_7, tbl_8, tbl_9, tbl_10, tbl_11, tbl_12, tbl_13, tbl_14, tbl_15, tbl_16, tbl_17, tbl_18, tbl_19, tbl_20, tbl_21, tbl_22, tbl_23, tbl_24, tbl_25, tbl_26, tbl_27, tbl_28, tbl_29, tbl_30, tbl_31, tbl_32, tbl_33, tbl_34, tbl_35, tbl_36, tbl_37, tbl_38, tbl_39, W_top1, b_top1, W_top2, b_top2, W_top3)
    dense_ctx, ids, tbl_0, tbl_1, tbl_2, tbl_3, tbl_4, tbl_5, tbl_6, tbl_7, tbl_8, tbl_9, tbl_10, tbl_11, tbl_12, tbl_13, tbl_14, tbl_15, tbl_16, tbl_17, tbl_18, tbl_19, tbl_20, tbl_21, tbl_22, tbl_23, tbl_24, tbl_25, tbl_26, tbl_27, tbl_28, tbl_29, tbl_30, tbl_31, tbl_32, tbl_33, tbl_34, tbl_35, tbl_36, tbl_37, tbl_38, tbl_39, W_top1, b_top1, W_top2, b_top2, W_top3 = _rec_inputs()

    def _L0_rec_setup():
        import jax, jax.numpy as jnp
        import numpy as np
        NUM_FIELDS = 40
        EMBED_DIM = 32
        BATCH = 512
        NUM_PAIRS = NUM_FIELDS * (NUM_FIELDS - 1) // 2
        key = jax.random.key(seed)
        k1, k2 = jax.random.split(key)
        inputs = jax.random.normal(k1, (BATCH, NUM_FIELDS, EMBED_DIM), dtype=jnp.float32)
        std = (2.0 / (EMBED_DIM + EMBED_DIM)) ** 0.5
        bilinear_matrices = jax.random.normal(k2, (NUM_PAIRS, EMBED_DIM, EMBED_DIM), dtype=jnp.float32) * std
        return {'inputs': inputs, 'bilinear_matrices': bilinear_matrices}
    _L0_rec_all = _L0_rec_setup()
    _L0_rec_in = {k: v for k, v in _L0_rec_all.items() if k in ('bilinear_matrices',)}
    del _L0_rec_all
    return {'dense_ctx': dense_ctx, 'ids': ids, 'tbl_0': tbl_0, 'tbl_1': tbl_1, 'tbl_2': tbl_2, 'tbl_3': tbl_3, 'tbl_4': tbl_4, 'tbl_5': tbl_5, 'tbl_6': tbl_6, 'tbl_7': tbl_7, 'tbl_8': tbl_8, 'tbl_9': tbl_9, 'tbl_10': tbl_10, 'tbl_11': tbl_11, 'tbl_12': tbl_12, 'tbl_13': tbl_13, 'tbl_14': tbl_14, 'tbl_15': tbl_15, 'tbl_16': tbl_16, 'tbl_17': tbl_17, 'tbl_18': tbl_18, 'tbl_19': tbl_19, 'tbl_20': tbl_20, 'tbl_21': tbl_21, 'tbl_22': tbl_22, 'tbl_23': tbl_23, 'tbl_24': tbl_24, 'tbl_25': tbl_25, 'tbl_26': tbl_26, 'tbl_27': tbl_27, 'tbl_28': tbl_28, 'tbl_29': tbl_29, 'tbl_30': tbl_30, 'tbl_31': tbl_31, 'tbl_32': tbl_32, 'tbl_33': tbl_33, 'tbl_34': tbl_34, 'tbl_35': tbl_35, 'tbl_36': tbl_36, 'tbl_37': tbl_37, 'tbl_38': tbl_38, 'tbl_39': tbl_39, 'W_top1': W_top1, 'b_top1': b_top1, 'W_top2': W_top2, 'b_top2': b_top2, 'W_top3': W_top3, 'L0_rec_bilinear_matrices': _L0_rec_in['bilinear_matrices']}

def reference(dense_ctx, ids, tbl_0, tbl_1, tbl_2, tbl_3, tbl_4, tbl_5, tbl_6, tbl_7, tbl_8, tbl_9, tbl_10, tbl_11, tbl_12, tbl_13, tbl_14, tbl_15, tbl_16, tbl_17, tbl_18, tbl_19, tbl_20, tbl_21, tbl_22, tbl_23, tbl_24, tbl_25, tbl_26, tbl_27, tbl_28, tbl_29, tbl_30, tbl_31, tbl_32, tbl_33, tbl_34, tbl_35, tbl_36, tbl_37, tbl_38, tbl_39, W_top1, b_top1, W_top2, b_top2, W_top3, L0_rec_bilinear_matrices):
    import jax
    import jax.numpy as jnp

    def _L0_rec_ref(inputs, bilinear_matrices):
        import jax, jax.numpy as jnp
        import numpy as np
        NUM_FIELDS = 40
        EMBED_DIM = 32
        BATCH = 512
        NUM_PAIRS = NUM_FIELDS * (NUM_FIELDS - 1) // 2
        num_fields = inputs.shape[1]
        iidx, jidx = jnp.triu_indices(num_fields, k=1)
        xi = inputs[:, iidx, :]
        xj = inputs[:, jidx, :]
        out = jnp.einsum('bpd,pde,bpe->bp', xi, bilinear_matrices, xj)
        return out
    e = jnp.stack([tbl_0[ids[:, 0]], tbl_1[ids[:, 1]], tbl_2[ids[:, 2]], tbl_3[ids[:, 3]], tbl_4[ids[:, 4]], tbl_5[ids[:, 5]], tbl_6[ids[:, 6]], tbl_7[ids[:, 7]], tbl_8[ids[:, 8]], tbl_9[ids[:, 9]], tbl_10[ids[:, 10]], tbl_11[ids[:, 11]], tbl_12[ids[:, 12]], tbl_13[ids[:, 13]], tbl_14[ids[:, 14]], tbl_15[ids[:, 15]], tbl_16[ids[:, 16]], tbl_17[ids[:, 17]], tbl_18[ids[:, 18]], tbl_19[ids[:, 19]], tbl_20[ids[:, 20]], tbl_21[ids[:, 21]], tbl_22[ids[:, 22]], tbl_23[ids[:, 23]], tbl_24[ids[:, 24]], tbl_25[ids[:, 25]], tbl_26[ids[:, 26]], tbl_27[ids[:, 27]], tbl_28[ids[:, 28]], tbl_29[ids[:, 29]], tbl_30[ids[:, 30]], tbl_31[ids[:, 31]], tbl_32[ids[:, 32]], tbl_33[ids[:, 33]], tbl_34[ids[:, 34]], tbl_35[ids[:, 35]], tbl_36[ids[:, 36]], tbl_37[ids[:, 37]], tbl_38[ids[:, 38]], tbl_39[ids[:, 39]]], axis=1)
    z = _L0_rec_ref(e, L0_rec_bilinear_matrices)
    z = z.reshape(z.shape[0], -1)
    h = jnp.concatenate([z, dense_ctx], axis=1)
    h = jnp.maximum(h @ W_top1 + b_top1, 0.0)
    h = jnp.maximum(h @ W_top2 + b_top2, 0.0)
    y = h @ W_top3
    return y

_drawn_inputs = setup_inputs


def setup_inputs(seed=0):
    import zlib

    import numpy as np

    out = dict(_drawn_inputs(seed))
    spreads = {'b_top1': (0.0, 0.1), 'b_top2': (0.0, 0.1)}
    factors = {'tbl_0': 3.704,
     'tbl_1': 3.172,
     'tbl_2': 3.43,
     'tbl_3': 2.856,
     'tbl_4': 3.14,
     'tbl_5': 2.919,
     'tbl_6': 3.229,
     'tbl_7': 3.428,
     'tbl_8': 2.954,
     'tbl_9': 3.058,
     'tbl_10': 3.258,
     'tbl_11': 3.574,
     'tbl_12': 2.974,
     'tbl_13': 3.109,
     'tbl_14': 3.019,
     'tbl_15': 3.233,
     'tbl_16': 3.286,
     'tbl_17': 3.249,
     'tbl_18': 3.375,
     'tbl_19': 3.219,
     'tbl_20': 2.944,
     'tbl_21': 3.303,
     'tbl_22': 3.203,
     'tbl_23': 3.095,
     'tbl_24': 3.319,
     'tbl_25': 3.318,
     'tbl_26': 2.992,
     'tbl_27': 3.328,
     'tbl_28': 3.032,
     'tbl_29': 3.071,
     'tbl_30': 3.295,
     'tbl_31': 3.026,
     'tbl_32': 3.316,
     'tbl_33': 3.293,
     'tbl_34': 3.105,
     'tbl_35': 3.047,
     'tbl_36': 3.652,
     'tbl_37': 3.404,
     'tbl_38': 3.448,
     'tbl_39': 3.19}
    for name, (base, spread) in spreads.items():
        noise = np.random.default_rng([zlib.crc32(name.encode()), seed]).standard_normal(out[name].shape)
        drawn = base * np.exp(spread * noise) if base else spread * noise
        out[name] = jnp.asarray(drawn.astype(out[name].dtype))
    for name, factor in factors.items():
        out[name] = (out[name] * factor).astype(out[name].dtype)
    return out
```

```python
from contextlib import ExitStack

import numpy as np

import concourse.bass as bass
from concourse import mybir

F32 = mybir.dt.float32
F32R = mybir.dt.float32r
I32 = mybir.dt.int32
ALU = mybir.AluOpType
ACT = mybir.ActivationFunctionType

P = 128
D = 32
FB = P // D
B = 512
BT = B // P
F = 40
NK = F // FB
F_PAIRS = F * (F - 1) // 2
DENSE = 16
N1, N2 = 512, 256
M1, M2 = N1 // P, N2 // P

ORDER = list(range(F))


def tile_plan():
    tiles = []
    for k in range(NK):
        for s in range(FB):
            targets = list(range(k if s == 0 else k + 1))
            tiles += [(k, s, i) for i in (targets if s % 2 == 0 else targets[::-1])]
    return tiles


TILES = tile_plan()
NT = len(TILES)
NG = NT // 2
assert NT % 2 == 0
NBURST = -(-NT // FB)
BPC = D // FB
NC = -(-NBURST // BPC)
SLOTS = NK * (NK + 1) // 2
LAST_GROUP = {}
FIRST_TILE = {}
for _t, (_k, _s, _i) in enumerate(TILES):
    LAST_GROUP[_k, _s] = _t // 2
    FIRST_TILE.setdefault((_k, _s), _t)

E_RING, W_RING, WS_RING, PROD_RING = 4, 2, 6, 4

SPLIT_AFTER = {8: 13, 9: 12}
TR_AFTER = {8: 14, 9: 14}


def step_plan():
    of_block = [[] for _ in range(NK)]
    for g in range(NG):
        of_block[TILES[2 * g + 1][0]].append(g)
    steps = []
    bursts = 0
    for k in range(NK):
        if ("split", k) not in steps:
            steps.append(("split", k))
        if ("transpose", k) not in steps:
            steps.append(("transpose", k))
        for n, g in enumerate(of_block[k]):
            steps.append(("group", g))
            while 2 * bursts + 1 <= g - 2:
                steps.append(("burst", bursts))
                bursts += 1
            if SPLIT_AFTER.get(k + 1, NG) == n:
                steps.append(("split", k + 1))
            if TR_AFTER.get(k + 1, NG) == n:
                steps.append(("transpose", k + 1))
    steps += [("burst", m) for m in range(bursts, NBURST)]
    return steps


STEPS = step_plan()


def z_row(t, target):
    m = t // FB
    return P * (m // BPC) + D * (t % FB) + FB * (m % BPC) + target


def dlrm_tower(nc, ids, tables, w_pairs, dense_t, w1, b1, w2, b2, w3, out):
    ctx = ExitStack()
    with ctx:
        def sb(name, shape, dt=F32):
            return ctx.enter_context(nc.sbuf_tensor(name, shape, dt))

        def sem(name):
            return ctx.enter_context(nc.semaphore(name))

        idx = sb("idx", [P, BT * F], I32)
        emb = sb("emb", [P, E_RING, BT, P])
        emb_hl = sb("emb_hl", [P, 2, BT * FB, 2, 2, D], F32R)
        xt = sb("xt", [P, NK, B])
        mov = sb("mov", [P, 2, FB, B], F32R)
        w_raw = sb("w_raw", [P, W_RING, NK * P])
        w_hi = sb("w_hi", [P, W_RING, NK * P], F32R)
        w_lo = sb("w_lo", [P, W_RING, NK * P], F32R)
        w_st = sb("w_st", [P, WS_RING, NK * P], F32R)
        prod = sb("prod", [P, PROD_RING, 2 * B])
        ones = sb("ones", [P, BPC * D])
        ident = sb("ident", [P, P])
        zt = sb("zt", [P, NC, B])
        dense_sb = sb("dense_sb", [DENSE, B])
        w1_sb = sb("w1_sb", [P, NC, N1])
        w1d_sb = sb("w1d_sb", [DENSE, N1])
        w2_sb = sb("w2_sb", [P, M1, N2])
        w3_sb = sb("w3_sb", [P, M2])
        b1_sb = sb("b1_sb", [P, M1])
        b2_sb = sb("b2_sb", [P, M2])
        h1 = sb("h1", [P, M1, B])
        h2 = sb("h2", [P, M2, B])
        y_sb = sb("y_sb", [1, B])

        ps_t = [ctx.enter_context(nc.psum_tensor(f"ps_t{n}", [P, 2 * B], F32)) for n in range(2)]
        ps_tr = [ctx.enter_context(nc.psum_tensor(f"ps_tr{n}", [P, B], F32)) for n in range(2)]
        ps_z = [ctx.enter_context(nc.psum_tensor(f"ps_z{n}", [P, B], F32)) for n in range(2)]

        ids_in = sem("ids_in")
        gathered = [sem(f"gathered{k}") for k in range(NK)]
        w_in = [sem(f"w_in{n}") for n in range(W_RING)]
        w_hi_made, w_lo_made = sem("w_hi_made"), sem("w_lo_made")
        restacked = [sem(f"restacked{n}") for n in range(WS_RING)]
        mlp_in = sem("mlp_in")
        ident_zero, ident_made = sem("ident_zero"), sem("ident_made")
        ones_zero, ones_made = sem("ones_zero"), sem("ones_made")
        x_hi_made, x_lo_made = sem("x_hi_made"), sem("x_lo_made")
        transposed = sem("transposed")
        moved = sem("moved")
        t_made = sem("t_made")
        multiplied = sem("multiplied")
        summed = sem("summed")
        z_moved = sem("z_moved")
        h1_made, h1_act, h1_dve = sem("h1_made"), sem("h1_act"), sem("h1_dve")
        h2_made, h2_act, h2_dve = sem("h2_made"), sem("h2_act"), sem("h2_dve")
        y_made, y_moved, y_out = sem("y_made"), sem("y_moved"), sem("y_out")

        block = ctx.enter_context(nc.Block())

        def slot0(k):
            return k * (k + 1) // 2

        def emb_twice(k):
            return emb[:, k % E_RING, :, :].rearrange("p t (f a d) -> p (t f) a d", a=1, d=D).broadcast_to([P, BT * FB, 2, D])

        @block.sync
        def _(sp):
            sp.dma_start(idx[:, :].rearrange("p (t f) -> p t f", t=BT),
                         ids.rearrange("(t p) f -> p t f", p=P)).then_inc(ids_in, 16)

            def load_weights(k):
                n = (k + 1) * P
                if k >= W_RING:
                    sp.wait_ge(w_hi_made, k - W_RING + 1)
                    sp.wait_ge(w_lo_made, k - W_RING + 1)
                sp.dma_start(w_raw[:, k % W_RING, 0:n],
                             w_pairs[:, slot0(k) * P:slot0(k) * P + n]).then_inc(w_in[k % W_RING], 16)

            for k in range(W_RING):
                load_weights(k)
            for k in range(NK):
                n = (k + 1) * P
                for s in range(FB):
                    stage = FB * k + s
                    slot = stage % WS_RING
                    if s == 0:
                        sp.wait_ge(w_hi_made, k + 1)
                        sp.wait_ge(w_lo_made, k + 1)
                    if stage >= WS_RING:
                        before = divmod(stage - WS_RING, FB)
                        if before in LAST_GROUP:
                            sp.wait_ge(t_made, LAST_GROUP[before] + 1)
                        else:
                            sp.wait_ge(restacked[slot], 64)
                    for c in range(4):
                        part = w_hi if c < 2 else w_lo
                        sp.dma_start(w_st[c * D:(c + 1) * D, slot, 0:n].bitcast(F32),
                                     part[s * D:(s + 1) * D, k % W_RING, 0:n].bitcast(F32)).then_inc(restacked[slot], 16)
                if k + W_RING < NK:
                    load_weights(k + W_RING)
                if k == 0:
                    sp.dma_start(w1_sb[:, :, :], w1[0:NC * P, :].rearrange("(c p) n -> p c n", p=P)).then_inc(mlp_in, 16)
                    sp.dma_start(w1d_sb[:, :], w1[NC * P:NC * P + DENSE, :]).then_inc(mlp_in, 16)
                    sp.dma_start(dense_sb[:, :], dense_t).then_inc(mlp_in, 16)
                    sp.dma_start(w2_sb[:, :, :], w2.rearrange("(c p) n -> p c n", p=P)).then_inc(mlp_in, 16)
                    sp.dma_start(w3_sb[:, :], w3).then_inc(mlp_in, 16)
                    sp.dma_start(b1_sb[:, :], b1).then_inc(mlp_in, 16)
                    sp.dma_start(b2_sb[:, :], b2).then_inc(mlp_in, 16)
            sp.wait_ge(y_moved, 1)
            sp.dma_start(out.rearrange("b o -> o b"), y_sb[:, :]).then_inc(y_out, 16)
            sp.wait_ge(y_out, 16)

        MLP_LOADS = 7 * 16

        @block.gpsimd
        def _(pool):
            nc.gpsimd.memset(ident[:, :], 0.0).then_inc(ident_zero, 1)
            pool.wait_ge(ident_zero, 1)
            nc.gpsimd.affine_select(out=ident[:, :], in_=ident[:, :], compare_op=ALU.not_equal, fill=1.0,
                                    base=0, pattern=[[-1, P]], channel_multiplier=1).then_inc(ident_made, 1)
            pool.wait_ge(ids_in, 16)
            for k in range(NK):
                if k >= E_RING:
                    pool.wait_ge(x_lo_made, k - E_RING + 1)
                    pool.wait_ge(transposed, (FB + 1) * (k - E_RING) + 1)
                for u in range(FB):
                    field = ORDER[FB * k + u]
                    for t in range(BT):
                        at = t * F + field
                        nc.gpsimd.indirect_dma_start(
                            emb[:, k % E_RING, t, u * D:(u + 1) * D], None, tables[field],
                            bass.IndirectOffsetOnAxis(ap=idx[:, at:at + 1], axis=0)).then_inc(gathered[k], 16)

        GATHERED = FB * BT * 16

        @block.scalar
        def _(act):
            def split_weights(k):
                act.wait_ge(w_in[k % W_RING], 16 * (k // W_RING + 1))
                if k >= W_RING:
                    for stage in range(FB * (k - W_RING), FB * (k - W_RING + 1)):
                        act.wait_ge(restacked[stage % WS_RING], 64 * (stage // WS_RING + 1))
                n = (k + 1) * P
                nc.scalar.activation(w_hi[:, k % W_RING, 0:n], w_raw[:, k % W_RING, 0:n], ACT.Copy).then_inc(w_hi_made, 1)

            for k in range(W_RING):
                split_weights(k)
            for what, k in STEPS:
                if what == "split":
                    act.wait_ge(gathered[k], GATHERED)
                    if k >= 2:
                        act.wait_ge(transposed, (FB + 1) * (k - 1))
                    nc.scalar.activation(emb_hl[:, k % 2, :, :, 0, :], emb_twice(k), ACT.Copy).then_inc(x_hi_made, 1)
                elif what == "transpose":
                    for u in range(FB + 1):
                        n = (FB + 1) * k + u
                        act.wait_ge(transposed, n + 1)
                        if u == 0:
                            o = xt[:, k, :]
                        else:
                            o = mov[:, k % 2, u - 1, :]
                            if (k - 2, u - 1) in LAST_GROUP:
                                act.wait_ge(t_made, LAST_GROUP[k - 2, u - 1] + 1)
                        nc.scalar.activation(o, ps_tr[n % 2][:, :], ACT.Copy).then_inc(moved, 1)
                    if 1 <= k and k + 1 < NK:
                        split_weights(k + 1)
                elif what == "burst" and (k % BPC == BPC - 1 or k == NBURST - 1):
                    c = k // BPC
                    act.wait_ge(summed, k + 1)
                    nc.scalar.activation(zt[:, c, :], ps_z[c % 2][:, :], ACT.Copy).then_inc(z_moved, 1)
            act.wait_ge(mlp_in, MLP_LOADS)
            for m in range(0, M1, 2):
                act.wait_ge(h1_made, m + 1)
                nc.scalar.activation(h1[:, m, :], ps_t[m // 2][:, 0:B], ACT.Relu, bias=b1_sb[:, m:m + 1]).then_inc(h1_act, 1)
            act.wait_ge(h2_made, 1)
            nc.scalar.activation(h2[:, 0, :], ps_tr[0][:, :], ACT.Relu, bias=b2_sb[:, 0:1]).then_inc(h2_act, 1)

        @block.vector
        def _(dve):
            nc.vector.memset(ones[:, :], 0.0).then_inc(ones_zero, 1)
            dve.wait_ge(ones_zero, 1)
            for g in range(FB):
                nc.vector.memset(ones[g * D:(g + 1) * D, g::D + FB], 1.0).then_inc(ones_made, 1)

            def split_weights(k):
                n = (k + 1) * P
                dve.wait_ge(w_hi_made, k + 1)
                if k >= W_RING:
                    for stage in range(FB * (k - W_RING), FB * (k - W_RING + 1)):
                        dve.wait_ge(restacked[stage % WS_RING], 64 * (stage // WS_RING + 1))
                nc.vector.tensor_tensor(w_lo[:, k % W_RING, 0:n], w_raw[:, k % W_RING, 0:n],
                                        w_hi[:, k % W_RING, 0:n].bitcast(F32), ALU.subtract).then_inc(w_lo_made, 1)

            for k in range(W_RING):
                split_weights(k)
            for what, k in STEPS:
                if what == "split":
                    dve.wait_ge(gathered[k], GATHERED)
                    dve.wait_ge(x_hi_made, k + 1)
                    if k >= 2:
                        dve.wait_ge(transposed, (FB + 1) * (k - 1))
                    nc.vector.tensor_tensor(emb_hl[:, k % 2, :, :, 1, :], emb_twice(k),
                                            emb_hl[:, k % 2, :, :, 0, :].bitcast(F32), ALU.subtract).then_inc(x_lo_made, 1)
                elif what == "transpose":
                    if 1 <= k and k + 1 < NK:
                        split_weights(k + 1)
                elif what == "group":
                    g = k
                    (ka, _, ia), (kb, _, ib) = TILES[2 * g], TILES[2 * g + 1]
                    if g == 0 or kb != TILES[2 * g - 1][0]:
                        dve.wait_ge(moved, (FB + 1) * kb + 1)
                    dve.wait_ge(t_made, g + 1)
                    if g >= PROD_RING:
                        dve.wait_ge(summed, (g - PROD_RING) // 2 + 1)
                    t_in = ps_t[g % 2][:, :].rearrange("p (i b) -> p i b", i=2)
                    o = prod[:, g % PROD_RING, :].rearrange("p (i b) -> p i b", i=2)
                    if ia == ib:
                        x_in = xt[:, ia:ia + 1, :].broadcast_to([P, 2, B])
                    else:
                        x_in = xt[:, min(ia, ib):max(ia, ib) + 1, :]
                    nc.vector.tensor_tensor(o, t_in, x_in, ALU.mult).then_inc(multiplied, 1)
            dve.wait_ge(mlp_in, MLP_LOADS)
            for m in range(1, M1, 2):
                dve.wait_ge(h1_made, m + 1)
                nc.vector.tensor_scalar(h1[:, m, :], ps_t[m // 2][:, B:2 * B], b1_sb[:, m:m + 1], 0.0,
                                        ALU.add, ALU.max).then_inc(h1_dve, 1)
            dve.wait_ge(h2_made, 2)
            nc.vector.tensor_scalar(h2[:, 1, :], ps_tr[1][:, :], b2_sb[:, 1:2], 0.0,
                                    ALU.add, ALU.max).then_inc(h2_dve, 1)
            dve.wait_ge(y_made, 1)
            nc.vector.tensor_copy(y_sb[:, :], ps_z[0][0:1, :]).then_inc(y_moved, 1)

        @block.tensor
        def _(pe):
            pe.wait_ge(ident_made, 1)
            for what, k in STEPS:
                if what == "transpose":
                    for u in range(FB + 1):
                        n = (FB + 1) * k + u
                        if u == 0:
                            pe.wait_ge(gathered[k], GATHERED)
                        if u == 1:
                            pe.wait_ge(x_hi_made, k + 1)
                            pe.wait_ge(x_lo_made, k + 1)
                        if n >= 2:
                            pe.wait_ge(moved, n - 1)
                        for t in range(BT):
                            if u == 0:
                                src = emb[:, k % E_RING, t, :]
                            else:
                                src = emb_hl[:, k % 2, t * FB + u - 1, :, :, :].rearrange("p a c d -> p (a c d)").bitcast(F32)
                            last = nc.tensor.transpose(ps_tr[n % 2][:, t * P:(t + 1) * P], src, ident[:, :])
                        last.then_inc(transposed, 1)
                elif what == "group":
                    g = k
                    if g >= 2:
                        pe.wait_ge(multiplied, g - 1)
                    (_, _, ia), (_, _, ib) = TILES[2 * g], TILES[2 * g + 1]
                    for t in (2 * g, 2 * g + 1):
                        kk, s, i = TILES[t]
                        stage = FB * kk + s
                        if t == FIRST_TILE[kk, s]:
                            pe.wait_ge(restacked[stage % WS_RING], 64 * (stage // WS_RING + 1))
                            pe.wait_ge(moved, (FB + 1) * kk + s + 2)
                        half = (t % 2) if ia <= ib else 1 - t % 2
                        last = nc.tensor.matmul(ps_t[g % 2][:, half * B:(half + 1) * B],
                                                w_st[:, stage % WS_RING, i * P:(i + 1) * P],
                                                mov[:, kk % 2, s, :], start=True, stop=True)
                    last.then_inc(t_made, 1)
                elif what == "burst":
                    m = k
                    if m == 0:
                        pe.wait_ge(ones_made, FB)
                    pe.wait_ge(multiplied, min(2 * m + 2, NG))
                    c, v = divmod(m, BPC)
                    if v == 0 and c >= 2:
                        pe.wait_ge(z_moved, c - 1)
                    for t in range(FB * m, min(FB * (m + 1), NT)):
                        q = t % FB
                        (_, _, ia), (_, _, ib) = TILES[t // 2 * 2], TILES[t // 2 * 2 + 1]
                        half = (t % 2) if ia <= ib else 1 - t % 2
                        last = nc.tensor.matmul(ps_z[c % 2][q * D:(q + 1) * D, :], ones[:, v * D:(v + 1) * D],
                                                prod[:, t // 2 % PROD_RING, half * B:(half + 1) * B],
                                                start=(v == 0), stop=(v == BPC - 1 or t + FB >= NT))
                    last.then_inc(summed, 1)
            pe.wait_ge(mlp_in, MLP_LOADS)
            pe.wait_ge(multiplied, NG)
            pe.wait_ge(z_moved, NC)
            for m in range(M1):
                o = ps_t[m // 2][:, (m % 2) * B:(m % 2 + 1) * B]
                nc.tensor.matmul(o, w1d_sb[:, m * P:(m + 1) * P], dense_sb[:, :], start=True, stop=False)
                for c in range(NC):
                    last = nc.tensor.matmul(o, w1_sb[:, c, m * P:(m + 1) * P], zt[:, c, :], start=False, stop=(c == NC - 1))
                last.then_inc(h1_made, 1)
            pe.wait_ge(moved, (FB + 1) * NK)
            pe.wait_ge(h1_act, M1 // 2)
            pe.wait_ge(h1_dve, M1 // 2)
            for m in range(M2):
                for c in range(M1):
                    last = nc.tensor.matmul(ps_tr[m][:, :], w2_sb[:, c, m * P:(m + 1) * P], h1[:, c, :],
                                            start=(c == 0), stop=(c == M1 - 1))
                last.then_inc(h2_made, 1)
            pe.wait_ge(h2_act, 1)
            pe.wait_ge(h2_dve, 1)
            for c in range(M2):
                last = nc.tensor.matmul(ps_z[0][0:1, :], w3_sb[:, c:c + 1], h2[:, c, :], start=(c == 0), stop=(c == M2 - 1))
            last.then_inc(y_made, 1)


def pair_index():
    i, j = np.triu_indices(F, k=1)
    at = np.zeros((F, F), np.int64)
    at[i, j] = np.arange(F_PAIRS)
    return at


def laid_out_weights(w):
    at = pair_index()
    o = np.zeros((FB, D, SLOTS, FB, D), w.dtype)
    for k in range(NK):
        for s in range(FB):
            src = ORDER[FB * k + s]
            for i in range(k + 1):
                for u in range(FB):
                    if FB * i + u < FB * k + s:
                        tgt = ORDER[FB * i + u]
                        m = w[at[tgt, src]].T if tgt < src else w[at[src, tgt]]
                        o[s, :, k * (k + 1) // 2 + i, u, :] = m
    return o.reshape(P, SLOTS * P)


def laid_out_w1(w1):
    at = pair_index()
    o = np.zeros((NC * P + DENSE, w1.shape[1]), w1.dtype)
    for t, (k, s, i) in enumerate(TILES):
        for u in range(FB):
            if FB * i + u < FB * k + s:
                a, b = sorted((ORDER[FB * i + u], ORDER[FB * k + s]))
                o[z_row(t, u)] = w1[at[a, b]]
    o[NC * P:] = w1[F_PAIRS:]
    return o


def kernel(**inputs):
    import concourse.bacc as bacc
    from concourse.bass_utils import run_bass_kernel_spmd

    a = {n: np.asarray(v) for n, v in inputs.items()}
    arrays = {
        "ids": a["ids"],
        "w_pairs": laid_out_weights(a["L0_rec_bilinear_matrices"]),
        "dense_t": np.ascontiguousarray(a["dense_ctx"].T),
        "w1": laid_out_w1(a["W_top1"]),
        "b1": np.ascontiguousarray(a["b_top1"].reshape(M1, P).T),
        "w2": a["W_top2"],
        "b2": np.ascontiguousarray(a["b_top2"].reshape(M2, P).T),
        "w3": np.ascontiguousarray(a["W_top3"].reshape(M2, P).T),
    }
    for f in range(F):
        arrays[f"tbl_{f}"] = a[f"tbl_{f}"]
    nc = bacc.Bacc("TRN2", target_bir_lowering=False, num_devices=1)
    ap = {n: nc.dram_tensor(n, v.shape, mybir.dt.from_np(v.dtype), kind="ExternalInput").ap() for n, v in arrays.items()}
    out = nc.dram_tensor("y", (B, 1), F32, kind="ExternalOutput").ap()
    dlrm_tower(nc, ap["ids"], [ap[f"tbl_{f}"] for f in range(F)], ap["w_pairs"], ap["dense_t"], ap["w1"], ap["b1"],
               ap["w2"], ap["b2"], ap["w3"], out)
    r = run_bass_kernel_spmd(nc, [arrays], core_ids=[0])
    return r.results[0]["y"]
```

```python
from contextlib import ExitStack

import numpy as np

import concourse.bass as bass
from concourse import mybir

F32 = mybir.dt.float32
F32R = mybir.dt.float32r
I32 = mybir.dt.int32
ALU = mybir.AluOpType
ACT = mybir.ActivationFunctionType

P = 128
D = 32
FB = P // D
B = 512
BT = B // P
F = 40
NK = F // FB
F_PAIRS = F * (F - 1) // 2
DENSE = 16
N1, N2 = 512, 256
M1, M2 = N1 // P, N2 // P

ROWS = [1250, 1250, 12500, 12500, 1250, 1000, 12500, 125000, 1250, 125000, 1000, 1000, 1000, 1000, 12500, 1000, 125000,
        12500, 12500, 1000, 125000, 1250, 125000, 1000, 1250, 12500, 1000, 1250, 125000, 12500, 12500, 1250, 1000, 1250,
        1250, 12500, 1000, 1250, 12500, 1000]
OH_BLOCKS = (0, 2, 4)
OH_ACT = 2
OH_ROWS = 1000
OH_CHUNKS = 8
OH_P = OH_ROWS // OH_CHUNKS
OH_FIELDS = [f for f in range(F) if ROWS[f] == OH_ROWS][:FB * len(OH_BLOCKS)]
OTHER_FIELDS = [f for f in range(F) if f not in OH_FIELDS]
ORDER = []
for _k in range(F // FB):
    _from = OH_FIELDS if _k in OH_BLOCKS else OTHER_FIELDS
    _n = len([f for f in ORDER if f in _from])
    ORDER += _from[_n:_n + FB]
assert sorted(ORDER) == list(range(F))


def tile_plan():
    tiles = []
    for k in range(NK):
        for s in range(FB):
            targets = list(range(k if s == 0 else k + 1))
            tiles += [(k, s, i) for i in (targets if s % 2 == 0 else targets[::-1])]
    return tiles


TILES = tile_plan()
NT = len(TILES)
NG = NT // 2
assert NT % 2 == 0
NBURST = -(-NT // FB)
BPC = D // FB
NC = -(-NBURST // BPC)
SLOTS = NK * (NK + 1) // 2
FIRST = 3
FIRST_COLS = [FB * P * k * (k + 1) // 2 for k in range(FIRST + 1)]
LAST_GROUP = {}
FIRST_TILE = {}
for _t, (_k, _s, _i) in enumerate(TILES):
    LAST_GROUP[_k, _s] = _t // 2
    FIRST_TILE.setdefault((_k, _s), _t)

E_RING, RAW_RING, W_RING, WS_RING, PROD_RING, OH_RING, MOV_RING = 3, 2, 3, 5, 4, 2, 2

XT_AFTER = {3: 1, 4: 5, 5: 4, 6: 3, 7: 9, 8: 8, 9: 6}
HOT_BEFORE = {('transpose', 0): [(0, 5), (2, 1), (0, 3)], ('transpose', 1): [(1, 1), (2, 1), (1, 2)], ('transpose', 2): [(1, 2), (2, 1), (1, 3)], ('group', 0): [(2, 1)], ('group', 5): [(2, 1)], ('group', 9): [(2, 1)], ('group', 11): [(2, 1)], ('group', 15): [(2, 1)]}
EARLY = [((0, 1), 37, 3), ((2, 3), 68, 4)]
LATE = [(4, 0), (4, 1), (4, 2), (5, 0), (5, 1), (5, 2), (4, 3), (5, 3), (6, 0), (6, 1), (6, 2), (6, 3)]
LATE_AFTER = {98: 1, 100: 1, 102: 2, 103: 1}
EARLY_MM = [(M1 * e + m, m, c, c == chunks[0], c == chunks[-1])
            for e, (chunks, _, _) in enumerate(EARLY) for m in range(M1) for c in chunks]


def step_plan():
    of_block = [[] for _ in range(NK)]
    for g in range(NG):
        of_block[TILES[2 * g + 1][0]].append(g)
    early_at = [first + pitch * j for chunks, first, pitch in EARLY for j in range(len(chunks) * M1)]
    steps = [("transpose", k) for k in range(3) if k not in XT_AFTER]
    bursts = 0
    early = late = 0
    for k in range(NK):
        for n, g in enumerate(of_block[k]):
            steps.append(("group", g))
            while 2 * bursts + 1 <= g - 2:
                steps.append(("burst", bursts))
                bursts += 1
            transpose_next = XT_AFTER.get(k + 1, NG) == n
            while early < len(early_at) and (early_at[early] <= g or (transpose_next and not EARLY_MM[early][3])):
                steps.append(("layer 1", early))
                early += 1
            for _ in range(LATE_AFTER.get(g, 0)):
                steps.append(("layer 1 late", late))
                late += 1
            if transpose_next:
                steps.append(("transpose", k + 1))
    steps += [("burst", m) for m in range(bursts, NBURST - 1)]
    steps += [("layer 1 late", n) for n in range(late, len(LATE)) if LATE[n][0] < NC - 1]
    steps.append(("burst", NBURST - 1))
    steps += [("layer 1 late", n) for n in range(late, len(LATE)) if LATE[n][0] == NC - 1]
    with_hot = []
    chunks = [0] * len(OH_BLOCKS)
    for step in steps:
        for j, n in HOT_BEFORE.get(step, []):
            with_hot += [("hot", (j, c)) for c in range(chunks[j], chunks[j] + n)]
            chunks[j] += n
        with_hot.append(step)
    for j, k in enumerate(OH_BLOCKS):
        at = with_hot.index(("hot", (j, OH_CHUNKS - 1)))
        assert at < with_hot.index(("transpose", k)) and (k == 0 or at > with_hot.index(("transpose", k - 1)))
    assert [j for what, j in with_hot if what == "layer 1"] == list(range(len(EARLY_MM)))
    return with_hot


STEPS = step_plan()
assert NK - OH_RING * FB >= OH_BLOCKS[OH_ACT - 1]


def t_pairs():
    begin = next(g for what, g in STEPS[STEPS.index(("transpose", OH_BLOCKS[OH_ACT])):] if what == "group")
    end = min(LATE_AFTER) + 1
    pair, before, last_in = [], [], {}
    ring = [0, 1]
    for g in range(NG):
        if g == begin:
            ring.append(2)
            last_in[2] = None
        if g >= end and 2 in ring:
            ring.remove(2)
        pair.append(ring.pop(0))
        ring.append(pair[-1])
        before.append(last_in.get(pair[-1]))
        last_in[pair[-1]] = g
    return pair, before, last_in[2]


PAIR, PAIR_BEFORE, LAST_IN_THIRD = t_pairs()


def shared_bank_waits():
    waits = {}
    blocks = units = 0
    open_unit = False
    for step in STEPS:
        what, k = step
        if what == "transpose":
            if k not in OH_BLOCKS[1:]:
                assert not open_unit
                waits[step] = (blocks, units)
            blocks = k + 1
        elif what == "layer 1":
            unit, _, _, first, last = EARLY_MM[k]
            if first:
                waits[step] = (blocks, units)
            open_unit = not last
            units = unit + 1
    return waits


SHARED_BANK_WAITS = shared_bank_waits()
FREE = FB * (NBURST - (NC - 1) * BPC)
DENSE_AT = [(0, FREE, 0, D - FREE), (1, FREE, D - FREE, DENSE - (D - FREE))]


def source_of(stage):
    return FIRST + stage // FB, stage % FB


def z_row(t, target):
    m = t // FB
    return P * (m // BPC) + D * (t % FB) + FB * (m % BPC) + target


def dlrm_tower(nc, ids, ids_oh_rows, small_tables, tables, first_weights, w_pairs, dense_t, w1, w2, vectors, out):
    ctx = ExitStack()
    with ctx:
        def sb(name, shape, dt=F32):
            return ctx.enter_context(nc.sbuf_tensor(name, shape, dt))

        def sem(name):
            return ctx.enter_context(nc.semaphore(name))

        idx = sb("idx", [P, BT * F], I32)
        emb = sb("emb", [P, E_RING, BT, P])
        tbl_oh = sb("tbl_oh", [P, len(OH_BLOCKS), FB, OH_CHUNKS, D])
        ramp = sb("ramp", [P, OH_CHUNKS])
        neg_ramp = sb("neg_ramp", [P, OH_CHUNKS])
        late_w = sb("late_w", [P, NC * N1 + M1 * N2])
        late_z = sb("late_z", [P, max(NC + M1, len(OH_FIELDS)) * B])
        hot_act = late_w[:, 0:OH_RING * FB * B].rearrange("p (r f b) -> p r f b", r=OH_RING, f=FB)
        w1_sb = late_w[:, 0:NC * N1].rearrange("p (c n) -> p c n", c=NC)
        w2_sb = late_w[:, NC * N1:NC * N1 + M1 * N2].rearrange("p (c n) -> p c n", c=M1)
        ids_oh = late_z[:, 0:len(OH_FIELDS) * B].rearrange("p (k f b) -> p k f b", f=FB, b=B)
        zt = late_z[:, 0:NC * B].rearrange("p (c b) -> p c b", c=NC)
        h1_part = late_z[:, NC * B:(NC + M1) * B].rearrange("p (m b) -> p m b", m=M1)
        x_part = sb("x_part", [P, 2, 2, B], F32R)
        xt = sb("xt", [P, NK, B])
        hot_dve = xt[:, NK - OH_RING * FB:, :].rearrange("p (r f) b -> p r f b", f=FB)
        mov = sb("mov", [P, MOV_RING, FB, B], F32R)
        n_small = len(OH_FIELDS)
        ids_raw = xt[0:n_small, 1, :].bitcast(I32)
        ids_r = mov[0:n_small, 1, 0, :]
        to_all = mov[0:n_small, 1, 1:FB, :].rearrange("q s b -> q (s b)").rearrange("q (f p) -> q f p", f=n_small)
        w_first = sb("w_first", [P, FIRST_COLS[FIRST]], F32R)
        w_raw = sb("w_raw", [P, RAW_RING, NK * P])
        w_hi = sb("w_hi", [P, W_RING, NK * P], F32R)
        w_lo = sb("w_lo", [P, W_RING, NK * P], F32R)
        w_st = sb("w_st", [P, WS_RING, NK * P], F32R)
        prod = sb("prod", [P, PROD_RING, 2 * B])
        w_first_raw = prod[:, :, :].rearrange("p r n -> p (r n)")[:, 0:FIRST_COLS[FIRST]]
        ones = sb("ones", [P, BPC * D])
        ident = sb("ident", [P, P])
        dense_sb = sb("dense_sb", [DENSE, B])
        put_dense = sb("put_dense", [DENSE, 2, D])
        vec_sb = sb("vec_sb", [P, M2 + M1 + M2])
        w3_sb, b1_sb, b2_sb = vec_sb[:, 0:M2], vec_sb[:, M2:M2 + M1], vec_sb[:, M2 + M1:]
        h1 = prod[:, 0:2, :].rearrange("p r (h b) -> p (r h) b", b=B)
        h2 = prod[:, 2, :].rearrange("p (h b) -> p h b", b=B)
        y_sb = prod[:, 3, 0:B // 4]

        ps_t = [ctx.enter_context(nc.psum_tensor(f"ps_t{n}", [P, 2 * B], F32)) for n in range(3)]
        ps_z = ctx.enter_context(nc.psum_tensor("ps_z", [P, B], F32))
        ps_x = ctx.enter_context(nc.psum_tensor("ps_x", [P, B], F32))
        ps_block = {OH_BLOCKS[1]: ps_t[1][:, 0:B], OH_BLOCKS[2]: ps_t[2][:, 0:B]}
        ps_late = [ps_t[2][:, 0:B], ps_t[2][:, B:2 * B], ps_x[:, :], ps_t[PAIR[NG - 2]][:, 0:B]]
        ps_h2 = [ps_t[PAIR[NG - 1]][:, m * B:(m + 1) * B] for m in range(M2)]
        Y_TILES = 4
        YB = B // Y_TILES

        ids_in = sem("ids_in")
        gathered = [sem(f"gathered{k}") for k in range(NK)]
        w_in = [sem(f"w_in{n}") for n in range(RAW_RING)]
        w_hi_made, w_lo_made = sem("w_hi_made"), sem("w_lo_made")
        first_in = [sem(f"first_in{k}") for k in range(FIRST)]
        first_hi_made, first_lo_made = sem("first_hi_made"), sem("first_lo_made")
        restacked = [sem(f"restacked{n}") for n in range(WS_RING)]
        mlp_in = sem("mlp_in")
        w1_in = {k: sem(f"w1_in{k}") for k in (5, 6, 7)}
        ident_zero, ident_made = sem("ident_zero"), sem("ident_made")
        ones_zero, ones_made = sem("ones_zero"), sem("ones_made")
        ramp_made, neg_ramp_made = sem("ramp_made"), sem("neg_ramp_made")
        ids_raw_in, ids_r_made, to_all_made = sem("ids_raw_in"), sem("ids_r_made"), sem("to_all_made")
        ids_spread = sem("ids_spread")
        ids_oh_made = sem("ids_oh_made")
        tbl_in = [sem(f"tbl_in{j}") for j in range(len(OH_BLOCKS))]
        hot_made_dve, hot_made_act = sem("hot_made_dve"), sem("hot_made_act")
        hot_used_dve, hot_used_act = sem("hot_used_dve"), sem("hot_used_act")
        distance_made = sem("distance_made")
        put_zero, put_made = sem("put_zero"), sem("put_made")
        h1_early, h1_kept = sem("h1_early"), sem("h1_kept")
        h1_added = sem("h1_added")
        x_hi_made, x_lo_made = sem("x_hi_made"), sem("x_lo_made")
        transposed = sem("transposed")
        moved = sem("moved")
        mov_in = [[sem(f"mov_in{n}_{s}") for s in range(FB)] for n in range(MOV_RING)]
        t_made = sem("t_made")
        multiplied = sem("multiplied")
        summed = sem("summed")
        z_moved = sem("z_moved")
        h1_made, h1_act = sem("h1_made"), sem("h1_act")
        h2_made, h2_act, h2_dve = sem("h2_made"), sem("h2_act"), sem("h2_dve")
        y_made, y_moved, y_out = sem("y_made"), sem("y_moved"), sem("y_out")

        block = ctx.enter_context(nc.Block())

        def slot0(k):
            return k * (k + 1) // 2 - FIRST * (FIRST + 1) // 2

        def parts_made(engine, k):
            engine.wait_ge(w_hi_made, k - FIRST + 1)
            engine.wait_ge(w_lo_made, k - FIRST + 1)

        MLP_LOADS = 3 * 16
        W1_LOADS = {5: (0, 2), 6: (2, 4), 7: (4, NC)}

        def part_read(engine, k):
            if k >= FIRST + W_RING:
                for stage in range(FB * (k - FIRST - W_RING), FB * (k - FIRST - W_RING + 1)):
                    engine.wait_ge(restacked[stage % WS_RING], 32 * (stage // WS_RING + 1))

        @block.sync
        def _(sp):
            def load_weights(k):
                n = (k + 1) * P
                if k >= FIRST + RAW_RING:
                    parts_made(sp, k - RAW_RING)
                sp.dma_start(w_raw[:, k % RAW_RING, 0:n],
                             w_pairs[:, slot0(k) * P:slot0(k) * P + n]).then_inc(w_in[k % RAW_RING], 16)

            def load_first_weights(k):
                cols = slice(FIRST_COLS[k], FIRST_COLS[k + 1])
                sp.dma_start(w_first_raw[:, cols], first_weights[:, cols]).then_inc(first_in[k], 16)

            def load_small_tables(j):
                sp.dma_start(tbl_oh[:, j, :, :, :].rearrange("p f c d -> p (f c d)"),
                             small_tables[j, :, :]).then_inc(tbl_in[j], 16)

            def restack_weights(stage):
                k, s = source_of(stage)
                n = (k + 1) * P
                slot = stage % WS_RING
                parts_made(sp, k)
                if stage >= WS_RING:
                    sp.wait_ge(t_made, LAST_GROUP[source_of(stage - WS_RING)] + 1)
                for half, part in ((0, w_hi), (1, w_lo)):
                    sp.dma_start(w_st[half * 2 * D:(half + 1) * 2 * D, slot, 0:n].bitcast(F32),
                                 part[s * D:(s + 1) * D, k % W_RING, 0:n].bitcast(F32).rearrange("p (a n) -> p a n", a=1)
                                 .broadcast_to([D, 2, n])).then_inc(restacked[slot], 16)

            def restack_sources(k):
                sp.wait_ge(x_hi_made, k + 1)
                sp.wait_ge(x_lo_made, k + 1)
                for s in range(FB):
                    if (k - MOV_RING, s) in LAST_GROUP:
                        sp.wait_ge(t_made, LAST_GROUP[k - MOV_RING, s] + 1)
                    elif k >= MOV_RING:
                        sp.wait_ge(mov_in[k % MOV_RING][s], 32)
                    for half in range(2):
                        sp.dma_start(mov[half * 2 * D:(half + 1) * 2 * D, k % MOV_RING, s, :].bitcast(F32),
                                     x_part[s * D:(s + 1) * D, k % 2, :, :].bitcast(F32)).then_inc(mov_in[k % MOV_RING][s], 16)

            sp.dma_start(ids_raw, ids_oh_rows).then_inc(ids_raw_in, 16)
            sp.dma_start(idx[:, :], ids).then_inc(ids_in, 16)
            load_small_tables(0)
            load_first_weights(0)
            load_small_tables(1)
            load_first_weights(1)
            load_small_tables(2)
            load_first_weights(2)
            load_weights(FIRST)
            load_weights(FIRST + 1)
            stages = 0
            for what, k in STEPS:
                if what == "transpose":
                    restack_sources(k)
                    if FIRST <= k < NK - RAW_RING:
                        load_weights(k + RAW_RING)
                    while stages < min(WS_RING, FB * (k - FIRST + 2)):
                        restack_weights(stages)
                        stages += 1
                    if k == OH_BLOCKS[OH_ACT] + 1:
                        sp.wait_ge(transposed, OH_BLOCKS[OH_ACT] + 1)
                        sp.dma_start(w2_sb, w2.rearrange("(c p) n -> p c n", p=P)).then_inc(mlp_in, 16)
                        sp.dma_start(dense_sb[:, :], dense_t).then_inc(mlp_in, 16)
                        sp.dma_start(vec_sb[:, :], vectors).then_inc(mlp_in, 16)
                    if k in W1_LOADS:
                        c0, c1 = W1_LOADS[k]
                        sp.dma_start(w1_sb[:, c0:c1, :], w1[c0 * P:c1 * P, :].rearrange("(c p) n -> p c n", p=P)).then_inc(w1_in[k], 16)
                elif what == "group":
                    while WS_RING <= stages < FB * (NK - FIRST) and LAST_GROUP[source_of(stages - WS_RING)] <= k:
                        restack_weights(stages)
                        stages += 1
            sp.wait_ge(y_moved, 1)
            sp.dma_start(out.rearrange("(q b) o -> q (o b)", q=Y_TILES), y_sb[0::D, :]).then_inc(y_out, 16)
            sp.wait_ge(y_out, 16)

        looked_up = [k for k in range(NK) if k not in OH_BLOCKS]

        @block.gpsimd
        def _(pool):
            nc.gpsimd.memset(ident[:, :], 0.0).then_inc(ident_zero, 1)
            pool.wait_ge(ident_zero, 1)
            nc.gpsimd.affine_select(out=ident[:, :], in_=ident[:, :], compare_op=ALU.not_equal, fill=1.0,
                                    base=0, pattern=[[-1, P]], channel_multiplier=1).then_inc(ident_made, 1)
            nc.gpsimd.iota(ramp[:, :], pattern=[[1, OH_CHUNKS]], base=0, channel_multiplier=OH_CHUNKS,
                           allow_small_or_imprecise_dtypes=True).then_inc(ramp_made, 1)
            pool.wait_ge(ids_in, 16)
            for n, k in enumerate(looked_up):
                if n >= E_RING:
                    pool.wait_ge(transposed, looked_up[n - E_RING] + 1)
                for u in range(FB):
                    field = ORDER[FB * k + u]
                    for t in range(BT):
                        at = t * F + field
                        nc.gpsimd.indirect_dma_start(
                            emb[:, n % E_RING, t, u * D:(u + 1) * D], None, tables[field],
                            bass.IndirectOffsetOnAxis(ap=idx[:, at:at + 1], axis=0)).then_inc(gathered[k], 16)

        GATHERED = FB * BT * 16

        @block.scalar
        def _(act):
            def split_weights(k):
                act.wait_ge(w_in[k % RAW_RING], 16 * ((k - FIRST) // RAW_RING + 1))
                part_read(act, k)
                n = (k + 1) * P
                nc.scalar.activation(w_hi[:, k % W_RING, 0:n], w_raw[:, k % RAW_RING, 0:n], ACT.Copy).then_inc(w_hi_made, 1)

            def split_first(k):
                cols = slice(FIRST_COLS[k], FIRST_COLS[k + 1])
                act.wait_ge(first_in[k], 16)
                nc.scalar.activation(w_first[:, cols], w_first_raw[:, cols], ACT.Copy).then_inc(first_hi_made, 1)

            def one_hot(c):
                if c == 0:
                    act.wait_ge(neg_ramp_made, 1)
                    act.wait_ge(ids_oh_made, 2 * OH_ACT + 2)
                if c >= OH_RING:
                    act.wait_ge(hot_used_act, c - OH_RING + 1)
                o = hot_act[:, c % OH_RING, :, :]
                nc.scalar.activation(o, ids_oh[:, OH_ACT, :, :], ACT.Abs, bias=neg_ramp[:, c:c + 1]).then_inc(distance_made, 1)
                act.wait_ge(distance_made, c + 1)
                nc.scalar.activation(o, o, ACT.Relu, bias=1.0, scale=-1.0).then_inc(hot_made_act, 1)

            for j in range(len(OH_BLOCKS)):
                for half in range(2):
                    act.wait_ge(ids_spread, 2 * j + half + 1)
                    nc.scalar.activation(ids_oh[:, j, 2 * half:2 * half + 2, :].rearrange("p f b -> p (f b)"), ps_t[half][:, :],
                                         ACT.Copy).then_inc(ids_oh_made, 1)
            for k in range(FIRST):
                split_first(k)
            one_hot(0)
            for what, k in STEPS:
                if what == "hot" and k[0] == OH_ACT and k[1] + 1 < OH_CHUNKS:
                    one_hot(k[1] + 1)
                if what == "transpose":
                    act.wait_ge(transposed, k + 1)
                    if k >= 2:
                        for s in range(FB):
                            act.wait_ge(mov_in[k % MOV_RING][s], 32 * (k // MOV_RING))
                    src = ps_block.get(k, ps_x[:, :])
                    nc.scalar.activation(x_part[:, k % 2, 0, :], src, ACT.Copy).then_inc(x_hi_made, 1)
                    nc.scalar.activation(xt[:, k, :], src, ACT.Copy).then_inc(moved, 1)
                    if 2 <= k < NK - 1:
                        split_weights(k + 1)
                elif what == "burst" and (k % BPC == BPC - 1 or k == NBURST - 1):
                    c = k // BPC
                    act.wait_ge(summed, k + 1)
                    nc.scalar.activation(zt[:, c, :], ps_z[:, :], ACT.Copy).then_inc(z_moved, 1)
                elif what == "layer 1" and EARLY_MM[k][4] and EARLY_MM[k][0] < M1:
                    unit = EARLY_MM[k][0]
                    act.wait_ge(mlp_in, MLP_LOADS)
                    act.wait_ge(h1_early, unit + 1)
                    nc.scalar.activation(h1_part[:, unit, :], ps_x[:, :], ACT.Identity, bias=b1_sb[:, unit:unit + 1]).then_inc(h1_kept, 1)
            for m in range(M1):
                act.wait_ge(h1_added, m + 1)
                nc.scalar.activation(h1[:, m, :], h1_part[:, m, :], ACT.Relu).then_inc(h1_act, 1)
            act.wait_ge(h2_made, 1)
            nc.scalar.activation(h2[:, 0, :], ps_h2[0], ACT.Relu, bias=b2_sb[:, 0:1]).then_inc(h2_act, 1)

        @block.vector
        def _(dve):
            dve.wait_ge(ident_made, 1)
            nc.vector.tensor_copy(to_all, ident[0:n_small, 0:n_small].rearrange("p (f a) -> p f a", a=1)
                                  .broadcast_to([n_small, n_small, P])).then_inc(to_all_made, 1)
            dve.wait_ge(ids_raw_in, 16)
            nc.vector.tensor_copy(ids_r, ids_raw).then_inc(ids_r_made, 1)
            nc.vector.memset(ones[:, :], 0.0).then_inc(ones_zero, 1)
            dve.wait_ge(ones_zero, 1)
            nc.vector.memset(put_dense[:, :, :], 0.0).then_inc(put_zero, 1)
            for g in range(FB):
                nc.vector.memset(ones[g * D:(g + 1) * D, g::D + FB], 1.0).then_inc(ones_made, 1)

            def split_weights(k):
                n = (k + 1) * P
                dve.wait_ge(w_hi_made, k - FIRST + 1)
                part_read(dve, k)
                nc.vector.tensor_tensor(w_lo[:, k % W_RING, 0:n], w_raw[:, k % RAW_RING, 0:n],
                                        w_hi[:, k % W_RING, 0:n].bitcast(F32), ALU.subtract).then_inc(w_lo_made, 1)

            def split_first(k):
                cols = slice(FIRST_COLS[k], FIRST_COLS[k + 1])
                dve.wait_ge(first_hi_made, k + 1)
                nc.vector.tensor_tensor(w_first[P // 2:, cols], w_first_raw[P // 2:, cols], w_first[P // 2:, cols].bitcast(F32),
                                        ALU.subtract).then_inc(first_lo_made, 1)

            dve.wait_ge(ramp_made, 1)
            nc.vector.tensor_scalar(neg_ramp[:, :], ramp[:, :], -1.0, None, ALU.mult).then_inc(neg_ramp_made, 1)
            dve.wait_ge(put_zero, 1)
            for q, row, first, n in DENSE_AT:
                nc.vector.tensor_copy(put_dense[:, q, row:row + n], ident[0:DENSE, first:first + n]).then_inc(put_made, 1)
            def one_hot(n):
                j, c = divmod(n, OH_CHUNKS)
                if c == 0:
                    dve.wait_ge(ids_oh_made, 2 * j + 2)
                before = n - OH_RING
                if before == OH_CHUNKS - 1:
                    dve.wait_ge(transposed, OH_BLOCKS[0] + 1)
                elif before >= 0:
                    dve.wait_ge(hot_used_dve, before + 1 - before // OH_CHUNKS)
                nc.vector.tensor_scalar(hot_dve[:, n % OH_RING, :, :], ids_oh[:, j, :, :],
                                        ramp[:, c:c + 1], None, ALU.is_equal).then_inc(hot_made_dve, 1)

            one_hot(0)
            for what, k in STEPS:
                if what == "hot" and k[0] < OH_ACT and k != (OH_ACT - 1, OH_CHUNKS - 1):
                    one_hot(k[0] * OH_CHUNKS + k[1] + 1)
                    if k in ((0, 2), (0, 4), (0, 6)):
                        split_first(k[1] // 2 - 1)
                if what == "transpose":
                    dve.wait_ge(x_hi_made, k + 1)
                    dve.wait_ge(moved, k + 1)
                    nc.vector.tensor_tensor(x_part[:, k % 2, 1, :], xt[:, k, :], x_part[:, k % 2, 0, :].bitcast(F32),
                                            ALU.subtract).then_inc(x_lo_made, 1)
                    if 2 <= k < NK - 1:
                        split_weights(k + 1)
                elif what == "group":
                    g = k
                    (ka, _, ia), (kb, _, ib) = TILES[2 * g], TILES[2 * g + 1]
                    if g == 0 or kb != TILES[2 * g - 1][0]:
                        dve.wait_ge(moved, kb + 1)
                    dve.wait_ge(t_made, g + 1)
                    if g >= PROD_RING:
                        dve.wait_ge(summed, (g - PROD_RING) // 2 + 1)
                    t_in = ps_t[PAIR[g]][:, :].rearrange("p (i b) -> p i b", i=2)
                    o = prod[:, g % PROD_RING, :].rearrange("p (i b) -> p i b", i=2)
                    if ia == ib:
                        x_in = xt[:, ia:ia + 1, :].broadcast_to([P, 2, B])
                    else:
                        x_in = xt[:, min(ia, ib):max(ia, ib) + 1, :]
                    nc.vector.tensor_tensor(o, t_in, x_in, ALU.mult).then_inc(multiplied, 1)
                elif what == "layer 1" and EARLY_MM[k][4] and EARLY_MM[k][0] >= M1:
                    unit, m = EARLY_MM[k][:2]
                    dve.wait_ge(h1_early, unit + 1)
                    dve.wait_ge(h1_kept, unit + 1 - M1)
                    nc.vector.tensor_tensor(h1_part[:, m, :], ps_x[:, :], h1_part[:, m, :], ALU.add).then_inc(h1_kept, 1)
            dve.wait_ge(h1_kept, M1 * len(EARLY))
            for m in range(M1):
                dve.wait_ge(h1_made, m + 1)
                nc.vector.tensor_tensor(h1_part[:, m, :], ps_late[m], h1_part[:, m, :],
                                        ALU.add).then_inc(h1_added, 1)
            dve.wait_ge(mlp_in, MLP_LOADS)
            dve.wait_ge(h2_made, 2)
            nc.vector.tensor_scalar(h2[:, 1, :], ps_h2[1], b2_sb[:, 1:2], 0.0,
                                    ALU.add, ALU.max).then_inc(h2_dve, 1)
            dve.wait_ge(y_made, 1)
            nc.vector.tensor_copy(y_sb, ps_z[:, 0:YB]).then_inc(y_moved, 1)

        @block.tensor
        def _(pe):
            pe.wait_ge(to_all_made, 1)
            pe.wait_ge(ids_r_made, 1)
            for j in range(len(OH_BLOCKS)):
                for half in range(2):
                    if j >= 1:
                        pe.wait_ge(ids_oh_made, 2 * (j - 1) + half + 1)
                    for f in range(2):
                        last = nc.tensor.matmul(ps_t[half][:, f * B:(f + 1) * B], to_all[:, FB * j + 2 * half + f, :],
                                                ids_r, start=True, stop=True)
                    last.then_inc(ids_spread, 1)
            for what, k in STEPS:
                if what == "hot":
                    j, c = k
                    hot, used = (hot_act, hot_used_act) if j == OH_ACT else (hot_dve, hot_used_dve)
                    bank = ps_block.get(OH_BLOCKS[j], ps_x[:, :])
                    if c == 0:
                        pe.wait_ge(tbl_in[j], 16)
                        if j == 1:
                            pe.wait_ge(ids_oh_made, 2 * len(OH_BLOCKS))
                    if j == OH_ACT:
                        pe.wait_ge(hot_made_act, c + 1)
                        slot = c % OH_RING
                    else:
                        pe.wait_ge(hot_made_dve, OH_CHUNKS * j + c + 1)
                        slot = (OH_CHUNKS * j + c) % OH_RING
                    if c == OH_CHUNKS - 1:
                        used = transposed
                    for s in range(FB):
                        last = nc.tensor.matmul(bank[s * D:(s + 1) * D, :], tbl_oh[:, j, s, c, :],
                                                hot[:, slot, s, :], start=(c == 0), stop=(c == OH_CHUNKS - 1))
                    last.then_inc(used, 1)
                elif what == "transpose" and k not in OH_BLOCKS:
                    blocks, units = SHARED_BANK_WAITS[what, k]
                    if blocks:
                        pe.wait_ge(moved, blocks)
                    if units:
                        pe.wait_ge(h1_kept, units)
                    pe.wait_ge(gathered[k], GATHERED)
                    for t in range(BT):
                        last = nc.tensor.transpose(ps_x[:, t * P:(t + 1) * P],
                                                   emb[:, looked_up.index(k) % E_RING, t, :], ident[:, :])
                    last.then_inc(transposed, 1)
                elif what == "group":
                    g = k
                    if PAIR_BEFORE[g] is not None:
                        pe.wait_ge(multiplied, PAIR_BEFORE[g] + 1)
                    elif PAIR[g] == 0:
                        pe.wait_ge(ids_oh_made, 2 * len(OH_BLOCKS))
                    else:
                        pe.wait_ge(moved, OH_BLOCKS[PAIR[g]] + 1)
                    (_, _, ia), (_, _, ib) = TILES[2 * g], TILES[2 * g + 1]
                    for t in (2 * g, 2 * g + 1):
                        kk, s, i = TILES[t]
                        if kk < FIRST:
                            at = FIRST_COLS[kk] + ((kk + 1) * s + i) * P
                            w_tile = w_first[:, at:at + P]
                        else:
                            stage = FB * (kk - FIRST) + s
                            w_tile = w_st[:, stage % WS_RING, i * P:(i + 1) * P]
                        if t == FIRST_TILE[kk, s]:
                            if kk < FIRST:
                                pe.wait_ge(first_hi_made, kk + 1)
                                pe.wait_ge(first_lo_made, kk + 1)
                            else:
                                pe.wait_ge(restacked[stage % WS_RING], 32 * (stage // WS_RING + 1))
                            pe.wait_ge(mov_in[kk % MOV_RING][s], 32 * (kk // MOV_RING + 1))
                        half = (t % 2) if ia <= ib else 1 - t % 2
                        last = nc.tensor.matmul(ps_t[PAIR[g]][:, half * B:(half + 1) * B],
                                                w_tile, mov[:, kk % MOV_RING, s, :], start=True, stop=True)
                    last.then_inc(t_made, 1)
                elif what == "burst":
                    m = k
                    if m == 0:
                        pe.wait_ge(ones_made, FB)
                    pe.wait_ge(multiplied, min(2 * m + 2, NG))
                    c, v = divmod(m, BPC)
                    if v == 0 and c >= 1:
                        pe.wait_ge(z_moved, c)
                    if v == 0 and c == NC - 1:
                        pe.wait_ge(put_made, len(DENSE_AT))
                        pe.wait_ge(mlp_in, MLP_LOADS)
                        for q, _, _, _ in DENSE_AT:
                            nc.tensor.matmul(ps_z[q * D:(q + 1) * D, :], put_dense[:, q, :], dense_sb[:, :], start=True, stop=False)
                    for t in range(FB * m, min(FB * (m + 1), NT)):
                        q = t % FB
                        (_, _, ia), (_, _, ib) = TILES[t // 2 * 2], TILES[t // 2 * 2 + 1]
                        half = (t % 2) if ia <= ib else 1 - t % 2
                        first = v == 0 and not (c == NC - 1 and q < len(DENSE_AT))
                        last = nc.tensor.matmul(ps_z[q * D:(q + 1) * D, :], ones[:, v * D:(v + 1) * D],
                                                prod[:, t // 2 % PROD_RING, half * B:(half + 1) * B],
                                                start=first, stop=(v == BPC - 1 or t + FB >= NT))
                    last.then_inc(summed, 1)
                elif what == "layer 1 late":
                    c, m = LATE[k]
                    if c == LATE[0][0]:
                        pe.wait_ge(w1_in[7], 16)
                        if m < 2:
                            pe.wait_ge(multiplied, LAST_IN_THIRD + 1)
                        elif m == 2:
                            pe.wait_ge(moved, NK)
                            pe.wait_ge(h1_kept, M1 * len(EARLY))
                        else:
                            pe.wait_ge(multiplied, NG - 1)
                    pe.wait_ge(z_moved, c + 1)
                    last = nc.tensor.matmul(ps_late[m], w1_sb[:, c, m * P:(m + 1) * P], zt[:, c, :],
                                            start=(c == LATE[0][0]), stop=(c == NC - 1))
                    if c == NC - 1:
                        last.then_inc(h1_made, 1)
                elif what == "layer 1":
                    unit, m, c, first, is_last = EARLY_MM[k]
                    if first:
                        pe.wait_ge(moved, SHARED_BANK_WAITS[what, k][0])
                        pe.wait_ge(w1_in[5 if c < 2 else 6], 16)
                        pe.wait_ge(z_moved, c + 2)
                        if unit >= 1:
                            pe.wait_ge(h1_kept, unit)
                    last = nc.tensor.matmul(ps_x[:, :], w1_sb[:, c, m * P:(m + 1) * P], zt[:, c, :], start=first, stop=is_last)
                    if is_last:
                        last.then_inc(h1_early, 1)
            pe.wait_ge(multiplied, NG)
            for c in range(M1):
                pe.wait_ge(h1_act, c + 1)
                for m in range(M2):
                    last = nc.tensor.matmul(ps_h2[m], w2_sb[:, c, m * P:(m + 1) * P], h1[:, c, :],
                                            start=(c == 0), stop=(c == M1 - 1))
                    if c == M1 - 1:
                        last.then_inc(h2_made, 1)
            pe.wait_ge(h2_act, 1)
            pe.wait_ge(h2_dve, 1)
            for c in range(M2):
                for q in range(Y_TILES):
                    last = nc.tensor.matmul(ps_z[q * D:q * D + 1, 0:YB], w3_sb[:, c:c + 1], h2[:, c, q * YB:(q + 1) * YB],
                                            start=(c == 0), stop=(c == M2 - 1), tile_position=(0, q * D))
            last.then_inc(y_made, 1)


def pair_index():
    i, j = np.triu_indices(F, k=1)
    at = np.zeros((F, F), np.int64)
    at[i, j] = np.arange(F_PAIRS)
    return at


def laid_out_weights(w):
    at = pair_index()
    o = np.zeros((FB, D, SLOTS, FB, D), w.dtype)
    for k in range(NK):
        for s in range(FB):
            src = ORDER[FB * k + s]
            for i in range(k + 1):
                for u in range(FB):
                    if FB * i + u < FB * k + s:
                        tgt = ORDER[FB * i + u]
                        m = w[at[tgt, src]].T if tgt < src else w[at[src, tgt]]
                        o[s, :, k * (k + 1) // 2 + i, u, :] = m
    n = FIRST * (FIRST + 1) // 2
    first = np.concatenate([o[:, :, k * (k + 1) // 2:(k + 1) * (k + 2) // 2].transpose(1, 0, 2, 3, 4).reshape(D, -1)
                            for k in range(FIRST)], axis=1)
    first = np.broadcast_to(first[None, :, None, :], (2, D, 2, first.shape[1])).reshape(P, -1)
    return np.ascontiguousarray(first), np.ascontiguousarray(o[:, :, n:].reshape(P, (SLOTS - n) * P))


def laid_out_w1(w1):
    at = pair_index()
    o = np.zeros((NC * P, w1.shape[1]), w1.dtype)
    for t, (k, s, i) in enumerate(TILES):
        for u in range(FB):
            if FB * i + u < FB * k + s:
                a, b = sorted((ORDER[FB * i + u], ORDER[FB * k + s]))
                o[z_row(t, u)] = w1[at[a, b]]
    for q, row, first, n in DENSE_AT:
        at_row = (NC - 1) * P + q * D + row
        o[at_row:at_row + n] = w1[F_PAIRS + first:F_PAIRS + first + n]
    return o


def laid_out_small_tables(tables):
    t = np.zeros((len(OH_BLOCKS), P, FB, OH_CHUNKS, D), tables[0].dtype)
    t[:, 0:OH_P] = np.stack(tables).reshape(len(OH_BLOCKS), FB, OH_P, OH_CHUNKS, D).transpose(0, 2, 1, 3, 4)
    return t.reshape(len(OH_BLOCKS), P, FB * OH_CHUNKS * D)


def kernel(**inputs):
    import concourse.bacc as bacc
    from concourse.bass_utils import run_bass_kernel_spmd

    a = {n: np.asarray(v) for n, v in inputs.items()}
    first_weights, w_pairs = laid_out_weights(a["L0_rec_bilinear_matrices"])
    arrays = {
        "ids": np.ascontiguousarray(a["ids"].reshape(BT, P, F).transpose(1, 0, 2)).reshape(P, BT * F),
        "ids_oh": np.ascontiguousarray(a["ids"].T[OH_FIELDS]),
        "small_tables": laid_out_small_tables([a[f"tbl_{f}"] for f in OH_FIELDS]),
        "first_weights": first_weights,
        "w_pairs": w_pairs,
        "dense_t": np.ascontiguousarray(a["dense_ctx"].T),
        "w1": laid_out_w1(a["W_top1"]),
        "w2": a["W_top2"],
        "vectors": np.concatenate([a["W_top3"].reshape(M2, P).T, a["b_top1"].reshape(M1, P).T, a["b_top2"].reshape(M2, P).T],
                                  axis=1),
    }
    for f in OTHER_FIELDS:
        arrays[f"tbl_{f}"] = a[f"tbl_{f}"]
    nc = bacc.Bacc("TRN2", target_bir_lowering=False, num_devices=1)
    ap = {n: nc.dram_tensor(n, v.shape, mybir.dt.from_np(v.dtype), kind="ExternalInput").ap() for n, v in arrays.items()}
    out = nc.dram_tensor("y", (B, 1), F32, kind="ExternalOutput").ap()
    dlrm_tower(nc, ap["ids"], ap["ids_oh"], ap["small_tables"], {f: ap[f"tbl_{f}"] for f in OTHER_FIELDS},
               ap["first_weights"], ap["w_pairs"],
               ap["dense_t"], ap["w1"], ap["w2"], ap["vectors"], out)
    r = run_bass_kernel_spmd(nc, [arrays], core_ids=[0])
    return r.results[0]["y"]
```

```python
from contextlib import ExitStack

import numpy as np

import concourse.bass as bass
from concourse import mybir

F32 = mybir.dt.float32
F32R = mybir.dt.float32r
I32 = mybir.dt.int32
ALU = mybir.AluOpType
ACT = mybir.ActivationFunctionType

P = 128
D = 32
FB = P // D
B = 512
BT = B // P
F = 40
NK = F // FB
F_PAIRS = F * (F - 1) // 2
DENSE = 16
N1, N2 = 512, 256
Y_TILES = FB
YB = B // Y_TILES
M1, M2 = N1 // P, N2 // P

ROWS = [1250, 1250, 12500, 12500, 1250, 1000, 12500, 125000, 1250, 125000, 1000, 1000, 1000, 1000, 12500, 1000, 125000,
        12500, 12500, 1000, 125000, 1250, 125000, 1000, 1250, 12500, 1000, 1250, 125000, 12500, 12500, 1250, 1000, 1250,
        1250, 12500, 1000, 1250, 12500, 1000]
OH_BLOCKS = (0, 2, 4)
OH_ACT = 2
DVE_HELPS = (6, 7)
OH_ROWS = 1000
OH_CHUNKS = 8
OH_P = OH_ROWS // OH_CHUNKS
OH_FIELDS = [f for f in range(F) if ROWS[f] == OH_ROWS][:FB * len(OH_BLOCKS)]
OTHER_FIELDS = [f for f in range(F) if f not in OH_FIELDS]
ORDER = []
for _k in range(F // FB):
    _from = OH_FIELDS if _k in OH_BLOCKS else OTHER_FIELDS
    _n = len([f for f in ORDER if f in _from])
    ORDER += _from[_n:_n + FB]
assert sorted(ORDER) == list(range(F))


OWN_TILES = (((3, FB),), ((1, FB), (0, 2), (2, 1)))
OWN_PAIRS = [(3, 0), (3, 1), (3, 2), (1, 2), (0, 1), (2, 0)]
assert sorted(tuple(sorted(p)) for p in OWN_PAIRS) == [(a, b) for a in range(FB) for b in range(a + 1, FB)]

FIRST = 3


def tile_plan():
    tiles = []
    for k in range(NK):
        own = [(k, parts, k) for parts in OWN_TILES]
        others = [(k, ((s, FB),), i) for s in range(FB) for i in list(range(k))[::1 if s % 2 == 0 else -1]]
        tiles += others + own
    return tiles


TILES = tile_plan()
NT = len(TILES)
NG = NT // 2
assert NT % 2 == 0
NBURST = -(-NT // FB)
BPC = D // FB
NC = -(-NBURST // BPC)
SLOTS = NK * (NK + 1) // 2
FIRST_COLS = [FB * P * k * (k + 1) // 2 for k in range(FIRST + 1)]
LAST_GROUP = {}
FIRST_TILE = {}
for _t, (_k, _parts, _i) in enumerate(TILES):
    for _s, _ in _parts:
        LAST_GROUP[_k, _s] = _t // 2
        FIRST_TILE.setdefault((_k, _s), _t)


def fields_of(t):
    k, parts, i = TILES[t]
    return [(u, ORDER[FB * k + s], ORDER[FB * i + u]) for s, n in parts for u in range(n)
            if i < k or (s, u) in OWN_PAIRS]


assert (sorted(tuple(sorted(p[1:])) for t in range(NT) for p in fields_of(t))
        == [(a, b) for a in range(F) for b in range(a + 1, F)])

E_RING, RAW_RING, W_RING, WS_RING, PROD_RING, OH_RING, MOV_RING = 3, 1, 2, 8, 4, 2, 2

XT_AFTER = {3: 2, 4: 3, 5: 4, 6: 7, 7: 8, 8: 7, 9: 2}
HOT_BEFORE = {("transpose", 0): [(0, 5), (2, 1), (0, 3), (1, 1)], ("transpose", 1): [(1, 1), (2, 1), (1, 3)],
              ("transpose", 2): [(2, 1), (1, 3)], ("group", 0): [(2, 1)], ("group", 4): [(2, 1)],
              ("group", 8): [(2, 2)], ("group", 12): [(2, 1)]}
EARLY = [((0, 1), 39, 3), ((2, 3), 67, 3)]
LATE = [(4, 0), (4, 1), (4, 2), (5, 0), (5, 1), (5, 2), (4, 3), (5, 3), (6, 0), (6, 1), (6, 2), (6, 3)]
LATE_AFTER = {92: 1, 94: 1, 96: 1}
W1_LOADS = {5: (0, 2), 6: (2, 4), 7: (4, NC)}
MLP_LOADS = 3 * 16
EARLY_MM = [(M1 * e + m, m, c, c == chunks[0], c == chunks[-1])
            for e, (chunks, _, _) in enumerate(EARLY) for m in range(M1) for c in chunks]


def step_plan():
    of_block = [[] for _ in range(NK)]
    for g in range(NG):
        of_block[TILES[2 * g + 1][0]].append(g)
    early_at = [first + pitch * j for chunks, first, pitch in EARLY for j in range(len(chunks) * M1)]
    steps = [("transpose", k) for k in range(3) if k not in XT_AFTER]
    bursts = 0
    early = late = 0
    for k in range(NK):
        for n, g in enumerate(of_block[k]):
            steps.append(("group", g))
            while 2 * bursts + 1 <= g - 2:
                steps.append(("burst", bursts))
                bursts += 1
            transpose_next = XT_AFTER.get(k + 1, NG) == n
            while early < len(early_at) and (early_at[early] <= g or (transpose_next and not EARLY_MM[early][3])):
                steps.append(("layer 1", early))
                early += 1
            for _ in range(LATE_AFTER.get(g, 0)):
                steps.append(("layer 1 late", late))
                late += 1
            if transpose_next:
                steps.append(("transpose", k + 1))
    steps += [("burst", m) for m in range(bursts, NBURST - 1)]
    steps += [("layer 1 late", n) for n in range(late, len(LATE)) if LATE[n][0] < NC - 1]
    steps.append(("burst", NBURST - 1))
    steps += [("layer 1 late", n) for n in range(late, len(LATE)) if LATE[n][0] == NC - 1]
    with_hot = []
    chunks = [0] * len(OH_BLOCKS)
    for step in steps:
        for j, n in HOT_BEFORE.get(step, []):
            with_hot += [("hot", (j, c)) for c in range(chunks[j], chunks[j] + n)]
            chunks[j] += n
        with_hot.append(step)
    for j, k in enumerate(OH_BLOCKS):
        at = with_hot.index(("hot", (j, OH_CHUNKS - 1)))
        assert at < with_hot.index(("transpose", k)) and (k == 0 or at > with_hot.index(("transpose", k - 1)))
    assert [j for what, j in with_hot if what == "layer 1"] == list(range(len(EARLY_MM)))
    return with_hot


STEPS = step_plan()
assert NK - OH_RING * FB >= OH_BLOCKS[OH_ACT - 1]


def t_pairs():
    begin = next(g for what, g in STEPS[STEPS.index(("transpose", OH_BLOCKS[OH_ACT])):] if what == "group")
    end = min(LATE_AFTER) + 1
    pair, before, last_in = [], [], {}
    ring = [0, 1]
    for g in range(NG):
        if g == begin:
            ring.append(2)
            last_in[2] = None
        if g >= end and 2 in ring:
            ring.remove(2)
        pair.append(ring.pop(0))
        ring.append(pair[-1])
        before.append(last_in.get(pair[-1]))
        last_in[pair[-1]] = g
    return pair, before, last_in[2]


PAIR, PAIR_BEFORE, LAST_IN_THIRD = t_pairs()


def shared_bank_waits():
    waits = {}
    blocks = units = 0
    open_unit = False
    for step in STEPS:
        what, k = step
        if what == "transpose":
            if k not in OH_BLOCKS[1:]:
                assert not open_unit
                waits[step] = (blocks, units)
            blocks = k + 1
        elif what == "layer 1":
            unit, _, _, first, last = EARLY_MM[k]
            if first:
                waits[step] = (blocks, units)
            open_unit = not last
            units = unit + 1
    return waits


SHARED_BANK_WAITS = shared_bank_waits()

FREE = FB * (NBURST - (NC - 1) * BPC)
DENSE_AT = [(0, FREE, 0, DENSE)]
assert NT == FB * NBURST and FREE + DENSE <= D


def source_of(stage):
    return FIRST + stage // FB, stage % FB


def z_row(t, target):
    m = t // FB
    return P * (m // BPC) + D * (t % FB) + FB * (m % BPC) + target


def dlrm_tower(nc, ids, ids_oh_rows, small_tables, tables, first_weights, w_pairs, dense_t, w1, w2, vectors, out):
    ctx = ExitStack()
    with ctx:
        def sb(name, shape, dt=F32):
            return ctx.enter_context(nc.sbuf_tensor(name, shape, dt))

        def sem(name):
            return ctx.enter_context(nc.semaphore(name))

        idx = sb("idx", [P, BT * F], I32)
        emb = sb("emb", [P, E_RING, BT, P])
        tbl_oh = sb("tbl_oh", [P, len(OH_BLOCKS), FB, OH_CHUNKS, D])
        ramp = sb("ramp", [P, OH_CHUNKS])
        neg_ramp = sb("neg_ramp", [P, OH_CHUNKS])
        late_w = sb("late_w", [P, NC * N1 + M1 * N2])
        late_z = sb("late_z", [P, max(NC + M1, len(OH_FIELDS)) * B])
        hot_act = late_w[:, 0:OH_RING * FB * B].rearrange("p (r f b) -> p r f b", r=OH_RING, f=FB)
        w1_sb = late_w[:, 0:NC * N1].rearrange("p (c n) -> p c n", c=NC)
        w2_sb = late_w[:, NC * N1:NC * N1 + M1 * N2].rearrange("p (c n) -> p c n", c=M1)
        ids_oh = late_z[:, 0:len(OH_FIELDS) * B].rearrange("p (k f b) -> p k f b", f=FB, b=B)
        zt = late_z[:, 0:NC * B].rearrange("p (c b) -> p c b", c=NC)
        h1_more = tbl_oh[:, :, :, :, :].rearrange("p j f c d -> p (j f c d)")[:, 0:M1 * B]
        h1_more = h1_more.rearrange("p (m b) -> p m b", m=M1)
        h1_part = late_z[:, NC * B:(NC + M1) * B].rearrange("p (m b) -> p m b", m=M1)
        x_part = sb("x_part", [P, 2, 2, B], F32R)
        xt = sb("xt", [P, NK, B])
        hot_dve = xt[:, NK - OH_RING * FB:, :].rearrange("p (r f) b -> p r f b", f=FB)
        mov = sb("mov", [P, MOV_RING, FB, B], F32R)
        n_small = len(OH_FIELDS)
        ids_raw = xt[0:n_small, 1, :].bitcast(I32)
        ids_r = mov[0:n_small, 1, 0, :]
        to_all = mov[0:n_small, 1, 1:FB, :].rearrange("q s b -> q (s b)").rearrange("q (f p) -> q f p", f=n_small)
        w_first = sb("w_first", [P, FIRST_COLS[FIRST]], F32R)
        w_raw = sb("w_raw", [P, RAW_RING, NK * P])
        w_hi = sb("w_hi", [P, W_RING, NK * P], F32R)
        w_lo = sb("w_lo", [P, W_RING, NK * P], F32R)
        w_st = sb("w_st", [P, WS_RING, NK * P], F32R)
        prod = sb("prod", [P, PROD_RING, 2 * B])
        w_first_raw = prod[:, :, :].rearrange("p r n -> p (r n)")[:, 0:FIRST_COLS[FIRST]]
        ones = sb("ones", [P, BPC * D])
        ident = sb("ident", [P, P])
        dense_sb = sb("dense_sb", [DENSE, B])
        put_dense = sb("put_dense", [DENSE, len(DENSE_AT), D])
        vec_sb = sb("vec_sb", [P, M2 + M1 + M2])
        w3_sb, b1_sb, b2_sb = vec_sb[:, 0:M2], vec_sb[:, M2:M2 + M1], vec_sb[:, M2 + M1:]
        h1 = prod[:, 0:2, :].rearrange("p r (h b) -> p (r h) b", b=B)
        h2 = prod[:, 2, :].rearrange("p (h b) -> p h b", b=B)
        y_sb = prod[:, 3, 0:YB]

        ps_t = [ctx.enter_context(nc.psum_tensor(f"ps_t{n}", [P, 2 * B], F32)) for n in range(3)]
        ps_z = ctx.enter_context(nc.psum_tensor("ps_z", [P, B], F32))
        ps_x = ctx.enter_context(nc.psum_tensor("ps_x", [P, B], F32))
        ps_block = {OH_BLOCKS[1]: ps_t[1][:, 0:B], OH_BLOCKS[2]: ps_t[2][:, 0:B]}
        ps_late = [ps_t[2][:, 0:B], ps_t[2][:, B:2 * B], ps_x[:, :], ps_t[PAIR[NG - 2]][:, 0:B]]
        ps_h2 = [ps_t[PAIR[NG - 1]][:, m * B:(m + 1) * B] for m in range(M2)]

        ids_in = sem("ids_in")
        gathered = [sem(f"gathered{k}") for k in range(NK)]
        w_in = [sem(f"w_in{n}") for n in range(RAW_RING)]
        w_hi_made, w_lo_made = sem("w_hi_made"), sem("w_lo_made")
        first_in = [sem(f"first_in{k}") for k in range(FIRST)]
        first_hi_made, first_lo_made = sem("first_hi_made"), sem("first_lo_made")
        restacked = [sem(f"restacked{n}") for n in range(WS_RING)]
        mlp_in = sem("mlp_in")
        w1_in = {chunks: sem(f"w1_in{chunks[0]}") for chunks in W1_LOADS.values()}
        ident_zero, ident_made = sem("ident_zero"), sem("ident_made")
        ones_zero, ones_made = sem("ones_zero"), sem("ones_made")
        ramp_made, neg_ramp_made = sem("ramp_made"), sem("neg_ramp_made")
        ids_raw_in, ids_r_made, to_all_made = sem("ids_raw_in"), sem("ids_r_made"), sem("to_all_made")
        ids_spread = sem("ids_spread")
        ids_oh_made = sem("ids_oh_made")
        tbl_in = [sem(f"tbl_in{j}") for j in range(len(OH_BLOCKS))]
        hot_made_dve, hot_made_act = sem("hot_made_dve"), sem("hot_made_act")
        hot_helped = sem("hot_helped")
        hot_used_dve, hot_used_act = sem("hot_used_dve"), sem("hot_used_act")
        distance_made = sem("distance_made")
        put_zero, put_made = sem("put_zero"), sem("put_made")
        h1_early, h1_kept = sem("h1_early"), sem("h1_kept")
        h1_joined = sem("h1_joined")
        h1_added = sem("h1_added")
        x_hi_made, x_lo_made = sem("x_hi_made"), sem("x_lo_made")
        transposed = sem("transposed")
        moved = sem("moved")
        mov_in = [[sem(f"mov_in{n}_{s}") for s in range(FB)] for n in range(MOV_RING)]
        t_made = sem("t_made")
        multiplied = sem("multiplied")
        summed = sem("summed")
        z_moved = sem("z_moved")
        h1_made, h1_act = sem("h1_made"), sem("h1_act")
        h2_made, h2_act, h2_dve = sem("h2_made"), sem("h2_act"), sem("h2_dve")
        y_made, y_moved, y_out = sem("y_made"), sem("y_moved"), sem("y_out")

        block = ctx.enter_context(nc.Block())

        def slot0(k):
            return k * (k + 1) // 2 - FIRST * (FIRST + 1) // 2

        def parts_made(engine, k):
            engine.wait_ge(w_hi_made, k - FIRST + 1)
            engine.wait_ge(w_lo_made, k - FIRST + 1)


        def part_read(engine, k):
            if k >= FIRST + W_RING:
                for stage in range(FB * (k - FIRST - W_RING), FB * (k - FIRST - W_RING + 1)):
                    engine.wait_ge(restacked[stage % WS_RING], 32 * (stage // WS_RING + 1))

        def act_chunks(c):
            return len([n for n in range(c + 1) if n not in DVE_HELPS])

        @block.sync
        def _(sp):
            def load_weights(k):
                n = (k + 1) * P
                if k >= FIRST + RAW_RING:
                    parts_made(sp, k - RAW_RING)
                sp.dma_start(w_raw[:, k % RAW_RING, 0:n],
                             w_pairs[:, slot0(k) * P:slot0(k) * P + n]).then_inc(w_in[k % RAW_RING], 16)

            def load_first_weights(k):
                cols = slice(FIRST_COLS[k], FIRST_COLS[k + 1])
                sp.dma_start(w_first_raw[:, cols], first_weights[:, cols]).then_inc(first_in[k], 16)

            def load_small_tables(j):
                sp.dma_start(tbl_oh[:, j, :, :, :].rearrange("p f c d -> p (f c d)"),
                             small_tables[j, :, :]).then_inc(tbl_in[j], 16)

            def restack_weights(stage):
                k, s = source_of(stage)
                n = (k + 1) * P
                slot = stage % WS_RING
                parts_made(sp, k)
                if stage >= WS_RING:
                    sp.wait_ge(t_made, LAST_GROUP[source_of(stage - WS_RING)] + 1)
                for half, part in ((0, w_hi), (1, w_lo)):
                    sp.dma_start(w_st[half * 2 * D:(half + 1) * 2 * D, slot, 0:n].bitcast(F32),
                                 part[s * D:(s + 1) * D, k % W_RING, 0:n].bitcast(F32).rearrange("p (a n) -> p a n", a=1)
                                 .broadcast_to([D, 2, n])).then_inc(restacked[slot], 16)

            def restack_sources(k):
                sp.wait_ge(x_hi_made, k + 1)
                sp.wait_ge(x_lo_made, k + 1)
                for s in range(FB):
                    if k >= MOV_RING:
                        sp.wait_ge(t_made, LAST_GROUP[k - MOV_RING, s] + 1)
                    for half in range(2):
                        sp.dma_start(mov[half * 2 * D:(half + 1) * 2 * D, k % MOV_RING, s, :].bitcast(F32),
                                     x_part[s * D:(s + 1) * D, k % 2, :, :].bitcast(F32)
                                     ).then_inc(mov_in[k % MOV_RING][s], 16)

            sp.dma_start(ids_raw, ids_oh_rows).then_inc(ids_raw_in, 16)
            sp.dma_start(idx[:, :], ids).then_inc(ids_in, 16)
            load_small_tables(0)
            load_first_weights(0)
            load_small_tables(1)
            load_first_weights(1)
            load_small_tables(2)
            load_first_weights(2)
            load_weights(FIRST)
            stages = 0
            groups_done = blocks_done = -1
            for what, k in STEPS:
                if what == "transpose":
                    restack_sources(k)
                    blocks_done = k
                    if k == OH_BLOCKS[OH_ACT] + 1:
                        sp.wait_ge(transposed, OH_BLOCKS[OH_ACT] + 1)
                        sp.dma_start(w2_sb, w2.rearrange("(c p) n -> p c n", p=P)).then_inc(mlp_in, 16)
                        sp.dma_start(dense_sb[:, :], dense_t).then_inc(mlp_in, 16)
                        sp.dma_start(vec_sb[:, :], vectors).then_inc(mlp_in, 16)
                    if k in W1_LOADS:
                        c0, c1 = W1_LOADS[k]
                        sp.dma_start(w1_sb[:, c0:c1, :],
                                     w1[c0 * P:c1 * P, :].rearrange("(c p) n -> p c n", p=P)).then_inc(w1_in[c0, c1], 16)
                elif what == "group":
                    groups_done = k
                if (what == "group" and stages < FB * (NK - FIRST) and source_of(stages)[0] <= blocks_done + 1
                        and (stages < WS_RING or LAST_GROUP[source_of(stages - WS_RING)] <= groups_done)):
                    restack_weights(stages)
                    stages += 1
                if what == "transpose" and FIRST <= k + 1 < NK - RAW_RING:
                    load_weights(k + 1 + RAW_RING)
            sp.wait_ge(y_moved, 1)
            sp.dma_start(out.rearrange("(q b) o -> q (o b)", q=Y_TILES), y_sb[0::D, :]).then_inc(y_out, 16)
            sp.wait_ge(y_out, 16)

        looked_up = [k for k in range(NK) if k not in OH_BLOCKS]

        @block.gpsimd
        def _(pool):
            nc.gpsimd.memset(ident[:, :], 0.0).then_inc(ident_zero, 1)
            pool.wait_ge(ident_zero, 1)
            nc.gpsimd.affine_select(out=ident[:, :], in_=ident[:, :], compare_op=ALU.not_equal, fill=1.0,
                                    base=0, pattern=[[-1, P]], channel_multiplier=1).then_inc(ident_made, 1)
            nc.gpsimd.iota(ramp[:, :], pattern=[[1, OH_CHUNKS]], base=0, channel_multiplier=OH_CHUNKS,
                           allow_small_or_imprecise_dtypes=True).then_inc(ramp_made, 1)
            pool.wait_ge(ids_in, 16)
            for n, k in enumerate(looked_up):
                if n >= E_RING:
                    pool.wait_ge(transposed, looked_up[n - E_RING] + 1)
                for u in range(FB):
                    field = ORDER[FB * k + u]
                    for t in range(BT):
                        at = t * F + field
                        nc.gpsimd.indirect_dma_start(
                            emb[:, n % E_RING, t, u * D:(u + 1) * D], None, tables[field],
                            bass.IndirectOffsetOnAxis(ap=idx[:, at:at + 1], axis=0)).then_inc(gathered[k], 16)
            for m in range(M1):
                pool.wait_ge(h1_kept, M1 * (len(EARLY) - 1) + m + 1)
                nc.gpsimd.tensor_tensor(h1_part[:, m, :], h1_part[:, m, :], h1_more[:, m, :],
                                        ALU.add).then_inc(h1_joined, 1)

        GATHERED = FB * BT * 16

        @block.scalar
        def _(act):
            def split_weights(k):
                act.wait_ge(w_in[k % RAW_RING], 16 * ((k - FIRST) // RAW_RING + 1))
                part_read(act, k)
                n = (k + 1) * P
                nc.scalar.activation(w_hi[:, k % W_RING, 0:n], w_raw[:, k % RAW_RING, 0:n], ACT.Copy).then_inc(w_hi_made, 1)

            def split_first(k):
                cols = slice(FIRST_COLS[k], FIRST_COLS[k + 1])
                act.wait_ge(first_in[k], 16)
                nc.scalar.activation(w_first[:, cols], w_first_raw[:, cols], ACT.Copy).then_inc(first_hi_made, 1)

            def one_hot(c):
                if c in DVE_HELPS:
                    return
                if c == 0:
                    act.wait_ge(neg_ramp_made, 1)
                    act.wait_ge(ids_oh_made, 2 * OH_ACT + 2)
                if c >= OH_RING:
                    act.wait_ge(hot_used_act, c - OH_RING + 1)
                o = hot_act[:, c % OH_RING, :, :]
                nc.scalar.activation(o, ids_oh[:, OH_ACT, :, :], ACT.Abs, bias=neg_ramp[:, c:c + 1]
                                     ).then_inc(distance_made, 1)
                act.wait_ge(distance_made, act_chunks(c))
                nc.scalar.activation(o, o, ACT.Relu, bias=1.0, scale=-1.0).then_inc(hot_made_act, 1)

            for j in range(len(OH_BLOCKS)):
                for half in range(2):
                    act.wait_ge(ids_spread, 2 * j + half + 1)
                    nc.scalar.activation(ids_oh[:, j, 2 * half:2 * half + 2, :].rearrange("p f b -> p (f b)"),
                                         ps_t[half][:, :], ACT.Copy).then_inc(ids_oh_made, 1)
            for k in range(FIRST):
                split_first(k)
            one_hot(0)
            for what, k in STEPS:
                if what == "hot" and k[0] == OH_ACT and k[1] + 1 < OH_CHUNKS:
                    one_hot(k[1] + 1)
                if what == "transpose":
                    act.wait_ge(transposed, k + 1)
                    if k >= 2:
                        for s in range(FB):
                            act.wait_ge(mov_in[k % MOV_RING][s], 32 * (k // MOV_RING))
                    src = ps_block.get(k, ps_x[:, :])
                    nc.scalar.activation(x_part[:, k % 2, 0, :], src, ACT.Copy).then_inc(x_hi_made, 1)
                    nc.scalar.activation(xt[:, k, :], src, ACT.Copy).then_inc(moved, 1)
                    if 2 <= k < NK - 1:
                        split_weights(k + 1)
                elif what == "burst" and (k % BPC == BPC - 1 or k == NBURST - 1):
                    c = k // BPC
                    act.wait_ge(summed, k + 1)
                    nc.scalar.activation(zt[:, c, :], ps_z[:, :], ACT.Copy).then_inc(z_moved, 1)
                elif what == "layer 1" and EARLY_MM[k][4]:
                    unit, m = EARLY_MM[k][:2]
                    act.wait_ge(mlp_in, MLP_LOADS)
                    act.wait_ge(h1_early, unit + 1)
                    if unit >= M1:
                        nc.scalar.activation(h1_more[:, m, :], ps_x[:, :], ACT.Copy).then_inc(h1_kept, 1)
                    else:
                        nc.scalar.activation(h1_part[:, unit, :], ps_x[:, :], ACT.Identity,
                                             bias=b1_sb[:, unit:unit + 1]).then_inc(h1_kept, 1)
            for m in range(M1):
                act.wait_ge(h1_added, m + 1)
                nc.scalar.activation(h1[:, m, :], h1_part[:, m, :], ACT.Relu).then_inc(h1_act, 1)
            act.wait_ge(h2_made, 1)
            nc.scalar.activation(h2[:, 0, :], ps_h2[0], ACT.Relu, bias=b2_sb[:, 0:1]).then_inc(h2_act, 1)

        @block.vector
        def _(dve):
            dve.wait_ge(ident_made, 1)
            nc.vector.tensor_copy(to_all, ident[0:n_small, 0:n_small].rearrange("p (f a) -> p f a", a=1)
                                  .broadcast_to([n_small, n_small, P])).then_inc(to_all_made, 1)
            dve.wait_ge(ids_raw_in, 16)
            nc.vector.tensor_copy(ids_r, ids_raw).then_inc(ids_r_made, 1)
            nc.vector.memset(ones[:, :], 0.0).then_inc(ones_zero, 1)
            dve.wait_ge(ones_zero, 1)
            nc.vector.memset(put_dense[:, :, :], 0.0).then_inc(put_zero, 1)
            for g in range(FB):
                nc.vector.memset(ones[g * D:(g + 1) * D, g::D + FB], 1.0).then_inc(ones_made, 1)

            def split_weights(k):
                n = (k + 1) * P
                dve.wait_ge(w_hi_made, k - FIRST + 1)
                part_read(dve, k)
                nc.vector.tensor_tensor(w_lo[:, k % W_RING, 0:n], w_raw[:, k % RAW_RING, 0:n],
                                        w_hi[:, k % W_RING, 0:n].bitcast(F32), ALU.subtract).then_inc(w_lo_made, 1)

            def split_first(k):
                cols = slice(FIRST_COLS[k], FIRST_COLS[k + 1])
                dve.wait_ge(first_hi_made, k + 1)
                nc.vector.tensor_tensor(w_first[P // 2:, cols], w_first_raw[P // 2:, cols],
                                        w_first[P // 2:, cols].bitcast(F32), ALU.subtract).then_inc(first_lo_made, 1)

            dve.wait_ge(ramp_made, 1)
            nc.vector.tensor_scalar(neg_ramp[:, :], ramp[:, :], -1.0, None, ALU.mult).then_inc(neg_ramp_made, 1)
            dve.wait_ge(put_zero, 1)
            for q, row, first, n in DENSE_AT:
                nc.vector.tensor_copy(put_dense[:, q, row:row + n], ident[0:DENSE, first:first + n]).then_inc(put_made, 1)

            def one_hot(n):
                j, c = divmod(n, OH_CHUNKS)
                if c == 0:
                    dve.wait_ge(ids_oh_made, 2 * j + 2)
                before = n - OH_RING
                if before == OH_CHUNKS - 1:
                    dve.wait_ge(transposed, OH_BLOCKS[0] + 1)
                elif before >= 0:
                    dve.wait_ge(hot_used_dve, before + 1 - before // OH_CHUNKS)
                nc.vector.tensor_scalar(hot_dve[:, n % OH_RING, :, :], ids_oh[:, j, :, :],
                                        ramp[:, c:c + 1], None, ALU.is_equal).then_inc(hot_made_dve, 1)

            def help_one_hot(c):
                dve.wait_ge(ids_oh_made, 2 * OH_ACT + 2)
                dve.wait_ge(hot_used_act, c - OH_RING + 1)
                nc.vector.tensor_scalar(hot_act[:, c % OH_RING, :, :], ids_oh[:, OH_ACT, :, :],
                                        ramp[:, c:c + 1], None, ALU.is_equal).then_inc(hot_helped, 1)

            one_hot(0)
            for what, k in STEPS:
                if what == "hot" and k[0] == OH_ACT and k[1] + 1 in DVE_HELPS:
                    help_one_hot(k[1] + 1)
                if what == "hot" and k[0] < OH_ACT and k != (OH_ACT - 1, OH_CHUNKS - 1):
                    one_hot(k[0] * OH_CHUNKS + k[1] + 1)
                    if k in ((0, 2), (0, 4), (0, 6)):
                        split_first(k[1] // 2 - 1)
                if what == "transpose":
                    dve.wait_ge(x_hi_made, k + 1)
                    dve.wait_ge(moved, k + 1)
                    nc.vector.tensor_tensor(x_part[:, k % 2, 1, :], xt[:, k, :], x_part[:, k % 2, 0, :].bitcast(F32),
                                            ALU.subtract).then_inc(x_lo_made, 1)
                    if 2 <= k < NK - 1:
                        split_weights(k + 1)
                elif what == "group":
                    g = k
                    (_, _, ia), (kb, _, ib) = TILES[2 * g], TILES[2 * g + 1]
                    if g == 0 or kb != TILES[2 * g - 1][0]:
                        dve.wait_ge(moved, kb + 1)
                    dve.wait_ge(t_made, g + 1)
                    if g >= PROD_RING:
                        dve.wait_ge(summed, (g - PROD_RING) // 2 + 1)
                    t_in = ps_t[PAIR[g]][:, :].rearrange("p (i b) -> p i b", i=2)
                    o = prod[:, g % PROD_RING, :].rearrange("p (i b) -> p i b", i=2)
                    if ia == ib:
                        x_in = xt[:, ia:ia + 1, :].broadcast_to([P, 2, B])
                    else:
                        x_in = xt[:, min(ia, ib):max(ia, ib) + 1, :]
                    nc.vector.tensor_tensor(o, t_in, x_in, ALU.mult).then_inc(multiplied, 1)
            dve.wait_ge(h1_joined, M1)
            for m in range(M1):
                dve.wait_ge(h1_made, m + 1)
                nc.vector.tensor_tensor(h1_part[:, m, :], ps_late[m], h1_part[:, m, :],
                                        ALU.add).then_inc(h1_added, 1)
            dve.wait_ge(mlp_in, MLP_LOADS)
            dve.wait_ge(h2_made, 2)
            nc.vector.tensor_scalar(h2[:, 1, :], ps_h2[1], b2_sb[:, 1:2], 0.0,
                                    ALU.add, ALU.max).then_inc(h2_dve, 1)
            dve.wait_ge(y_made, 1)
            nc.vector.tensor_copy(y_sb, ps_z[:, 0:YB]).then_inc(y_moved, 1)

        @block.tensor
        def _(pe):
            pe.wait_ge(to_all_made, 1)
            pe.wait_ge(ids_r_made, 1)
            for j in range(len(OH_BLOCKS)):
                for half in range(2):
                    if j >= 1:
                        pe.wait_ge(ids_oh_made, 2 * (j - 1) + half + 1)
                    for f in range(2):
                        last = nc.tensor.matmul(ps_t[half][:, f * B:(f + 1) * B], to_all[:, FB * j + 2 * half + f, :],
                                                ids_r, start=True, stop=True)
                    last.then_inc(ids_spread, 1)
            for what, k in STEPS:
                if what == "hot":
                    j, c = k
                    hot, used = (hot_act, hot_used_act) if j == OH_ACT else (hot_dve, hot_used_dve)
                    bank = ps_block.get(OH_BLOCKS[j], ps_x[:, :])
                    if c == 0:
                        pe.wait_ge(tbl_in[j], 16)
                        if j == 1:
                            pe.wait_ge(ids_oh_made, 2 * len(OH_BLOCKS))
                    if j == OH_ACT:
                        if c in DVE_HELPS:
                            pe.wait_ge(hot_helped, c + 1 - act_chunks(c))
                        else:
                            pe.wait_ge(hot_made_act, act_chunks(c))
                        slot = c % OH_RING
                    else:
                        pe.wait_ge(hot_made_dve, OH_CHUNKS * j + c + 1)
                        slot = (OH_CHUNKS * j + c) % OH_RING
                    if c == OH_CHUNKS - 1:
                        used = transposed
                    for s in range(FB):
                        last = nc.tensor.matmul(bank[s * D:(s + 1) * D, :], tbl_oh[:, j, s, c, :],
                                                hot[:, slot, s, :], start=(c == 0), stop=(c == OH_CHUNKS - 1))
                    last.then_inc(used, 1)
                elif what == "transpose" and k not in OH_BLOCKS:
                    blocks, units = SHARED_BANK_WAITS[what, k]
                    if blocks:
                        pe.wait_ge(moved, blocks)
                    if units:
                        pe.wait_ge(h1_kept, units)
                    pe.wait_ge(gathered[k], GATHERED)
                    for t in range(BT):
                        last = nc.tensor.transpose(ps_x[:, t * P:(t + 1) * P],
                                                   emb[:, looked_up.index(k) % E_RING, t, :], ident[:, :])
                    last.then_inc(transposed, 1)
                elif what == "group":
                    g = k
                    if PAIR_BEFORE[g] is not None:
                        pe.wait_ge(multiplied, PAIR_BEFORE[g] + 1)
                    elif PAIR[g] == 0:
                        pe.wait_ge(ids_oh_made, 2 * len(OH_BLOCKS))
                    else:
                        pe.wait_ge(moved, OH_BLOCKS[PAIR[g]] + 1)
                    (_, _, ia), (_, _, ib) = TILES[2 * g], TILES[2 * g + 1]
                    for t in (2 * g, 2 * g + 1):
                        kk, parts, i = TILES[t]
                        half = (t % 2) if ia <= ib else 1 - t % 2
                        for s, n in parts:
                            if kk < FIRST:
                                w_tiles, at = w_first, FIRST_COLS[kk] + (kk + 1) * s * P
                            else:
                                stage = FB * (kk - FIRST) + s
                                w_tiles, at = w_st[:, stage % WS_RING, :], 0
                            if t == FIRST_TILE[kk, s]:
                                if kk < FIRST:
                                    pe.wait_ge(first_hi_made, kk + 1)
                                    pe.wait_ge(first_lo_made, kk + 1)
                                else:
                                    pe.wait_ge(restacked[stage % WS_RING], 32 * (stage // WS_RING + 1))
                                pe.wait_ge(mov_in[kk % MOV_RING][s], 32 * (kk // MOV_RING + 1))
                            at += i * P
                            last = nc.tensor.matmul(ps_t[PAIR[g]][0:n * D, half * B:(half + 1) * B],
                                                    w_tiles[:, at:at + n * D], mov[:, kk % MOV_RING, s, :],
                                                    start=True, stop=True)
                    last.then_inc(t_made, 1)
                elif what == "burst":
                    m = k
                    if m == 0:
                        pe.wait_ge(ones_made, FB)
                    pe.wait_ge(multiplied, min(2 * m + 2, NG))
                    c, v = divmod(m, BPC)
                    if v == 0 and c >= 1:
                        pe.wait_ge(z_moved, c)
                    if v == 0 and c == NC - 1:
                        pe.wait_ge(put_made, len(DENSE_AT))
                        pe.wait_ge(mlp_in, MLP_LOADS)
                        for q, _, _, _ in DENSE_AT:
                            nc.tensor.matmul(ps_z[q * D:(q + 1) * D, :], put_dense[:, q, :], dense_sb[:, :],
                                             start=True, stop=False)
                    for t in range(FB * m, min(FB * (m + 1), NT)):
                        q = t % FB
                        (_, _, ia), (_, _, ib) = TILES[t // 2 * 2], TILES[t // 2 * 2 + 1]
                        half = (t % 2) if ia <= ib else 1 - t % 2
                        first = v == 0 and not (c == NC - 1 and q < len(DENSE_AT))
                        last = nc.tensor.matmul(ps_z[q * D:(q + 1) * D, :], ones[:, v * D:(v + 1) * D],
                                                prod[:, t // 2 % PROD_RING, half * B:(half + 1) * B],
                                                start=first, stop=(v == BPC - 1 or t + FB >= NT))
                    last.then_inc(summed, 1)
                elif what == "layer 1 late":
                    c, m = LATE[k]
                    if c == LATE[0][0]:
                        pe.wait_ge(w1_in[W1_LOADS[7]], 16)
                        if m < 2:
                            pe.wait_ge(multiplied, LAST_IN_THIRD + 1)
                        elif m == 2:
                            pe.wait_ge(moved, NK)
                            pe.wait_ge(h1_kept, M1 * len(EARLY))
                        else:
                            pe.wait_ge(multiplied, NG - 1)
                    pe.wait_ge(z_moved, c + 1)
                    last = nc.tensor.matmul(ps_late[m], w1_sb[:, c, m * P:(m + 1) * P], zt[:, c, :],
                                            start=(c == LATE[0][0]), stop=(c == NC - 1))
                    if c == NC - 1:
                        last.then_inc(h1_made, 1)
                elif what == "layer 1":
                    unit, m, c, first, is_last = EARLY_MM[k]
                    if first:
                        pe.wait_ge(moved, SHARED_BANK_WAITS[what, k][0])
                        pe.wait_ge(w1_in[W1_LOADS[5] if c < 2 else W1_LOADS[6]], 16)
                        if unit >= 1:
                            pe.wait_ge(h1_kept, unit)
                    pe.wait_ge(z_moved, c + 1)
                    last = nc.tensor.matmul(ps_x[:, :], w1_sb[:, c, m * P:(m + 1) * P], zt[:, c, :],
                                            start=first, stop=is_last)
                    if is_last:
                        last.then_inc(h1_early, 1)
            pe.wait_ge(multiplied, NG)
            for c in range(M1):
                pe.wait_ge(h1_act, c + 1)
                for m in range(M2):
                    last = nc.tensor.matmul(ps_h2[m], w2_sb[:, c, m * P:(m + 1) * P], h1[:, c, :],
                                            start=(c == 0), stop=(c == M1 - 1))
                    if c == M1 - 1:
                        last.then_inc(h2_made, 1)
            pe.wait_ge(h2_act, 1)
            pe.wait_ge(h2_dve, 1)
            for c in range(M2):
                for q in range(Y_TILES):
                    last = nc.tensor.matmul(ps_z[q * D:q * D + 1, 0:YB], w3_sb[:, c:c + 1], h2[:, c, q * YB:(q + 1) * YB],
                                            start=(c == 0), stop=(c == M2 - 1), tile_position=(0, q * D))
            last.then_inc(y_made, 1)


def pair_index():
    i, j = np.triu_indices(F, k=1)
    at = np.zeros((F, F), np.int64)
    at[i, j] = np.arange(F_PAIRS)
    return at


def laid_out_weights(w):
    at = pair_index()
    o = np.zeros((FB, D, SLOTS, FB, D), w.dtype)
    for k in range(NK):
        for s in range(FB):
            src = ORDER[FB * k + s]
            for i in range(k + 1):
                for u in range(FB):
                    if i < k or (s, u) in OWN_PAIRS:
                        tgt = ORDER[FB * i + u]
                        m = w[at[tgt, src]].T if tgt < src else w[at[src, tgt]]
                        o[s, :, k * (k + 1) // 2 + i, u, :] = m
    n = FIRST * (FIRST + 1) // 2
    first = np.concatenate([o[:, :, k * (k + 1) // 2:(k + 1) * (k + 2) // 2].transpose(1, 0, 2, 3, 4).reshape(D, -1)
                            for k in range(FIRST)], axis=1)
    first = np.broadcast_to(first[None, :, None, :], (2, D, 2, first.shape[1])).reshape(P, -1)
    return np.ascontiguousarray(first), np.ascontiguousarray(o[:, :, n:].reshape(P, (SLOTS - n) * P))


def laid_out_w1(w1):
    at = pair_index()
    o = np.zeros((NC * P, w1.shape[1]), w1.dtype)
    for t in range(NT):
        for u, src, tgt in fields_of(t):
            o[z_row(t, u)] = w1[at[min(src, tgt), max(src, tgt)]]
    for q, row, first, n in DENSE_AT:
        at_row = (NC - 1) * P + q * D + row
        o[at_row:at_row + n] = w1[F_PAIRS + first:F_PAIRS + first + n]
    return o


def laid_out_small_tables(tables):
    t = np.zeros((len(OH_BLOCKS), P, FB, OH_CHUNKS, D), tables[0].dtype)
    t[:, 0:OH_P] = np.stack(tables).reshape(len(OH_BLOCKS), FB, OH_P, OH_CHUNKS, D).transpose(0, 2, 1, 3, 4)
    return t.reshape(len(OH_BLOCKS), P, FB * OH_CHUNKS * D)


def kernel(**inputs):
    import concourse.bacc as bacc
    from concourse.bass_utils import run_bass_kernel_spmd

    a = {n: np.asarray(v) for n, v in inputs.items()}
    first_weights, w_pairs = laid_out_weights(a["L0_rec_bilinear_matrices"])
    arrays = {
        "ids": np.ascontiguousarray(a["ids"].reshape(BT, P, F).transpose(1, 0, 2)).reshape(P, BT * F),
        "ids_oh": np.ascontiguousarray(a["ids"].T[OH_FIELDS]),
        "small_tables": laid_out_small_tables([a[f"tbl_{f}"] for f in OH_FIELDS]),
        "first_weights": first_weights,
        "w_pairs": w_pairs,
        "dense_t": np.ascontiguousarray(a["dense_ctx"].T),
        "w1": laid_out_w1(a["W_top1"]),
        "w2": a["W_top2"],
        "vectors": np.concatenate([a["W_top3"].reshape(M2, P).T, a["b_top1"].reshape(M1, P).T,
                                   a["b_top2"].reshape(M2, P).T], axis=1),
    }
    for f in OTHER_FIELDS:
        arrays[f"tbl_{f}"] = a[f"tbl_{f}"]
    nc = bacc.Bacc("TRN2", target_bir_lowering=False, num_devices=1)
    ap = {n: nc.dram_tensor(n, v.shape, mybir.dt.from_np(v.dtype), kind="ExternalInput").ap() for n, v in arrays.items()}
    out = nc.dram_tensor("y", (B, 1), F32, kind="ExternalOutput").ap()
    dlrm_tower(nc, ap["ids"], ap["ids_oh"], ap["small_tables"], {f: ap[f"tbl_{f}"] for f in OTHER_FIELDS},
               ap["first_weights"], ap["w_pairs"],
               ap["dense_t"], ap["w1"], ap["w2"], ap["vectors"], out)
    r = run_bass_kernel_spmd(nc, [arrays], core_ids=[0])
    return r.results[0]["y"]
```
